# Optimizing a Trainium2 kernel written in Bass

```python
import numpy as np
import jax
import jax.numpy as jnp

def _softmax(x, axis=-1):
    return jax.nn.softmax(x, axis=axis)

def _gelu(x):
    return jax.nn.gelu(x, approximate=True)

def _silu(x):
    return jax.nn.silu(x)

def _sigmoid(x):
    return jax.nn.sigmoid(x)

def _layernorm(x, axis=-1, eps=1e-05):
    m = jnp.mean(x, axis=axis, keepdims=True)
    v = jnp.var(x, axis=axis, keepdims=True)
    return (x - m) / jnp.sqrt(v + eps)

def _scatter_add(tgt, idx, src, axis=0):
    return tgt.at[idx].add(src)

def _segment_sum(src, seg, n):
    return jax.ops.segment_sum(src, seg, n)
kernel_name = 'mk_prb_d1_jaxref_r8_7a0c65'

def setup_inputs(seed: int=0):
    np.random.seed(seed)
    _w = jnp.asarray

    def _L0_attn_setup():
        import jax, jax.numpy as jnp
        import numpy as np
        H = 16
        RMS_EPS = 1.1920928955078125e-07
        NORM_EPS = 1e-12

        def _rms_norm(t):
            ms = jnp.mean(t * t, axis=-1, keepdims=True)
            return t * jax.lax.rsqrt(ms + RMS_EPS)
        key = jax.random.key(seed)
        k1, k2, k3 = jax.random.split(key, 3)
        B, N, C = (2, 256, 128)
        x = jax.random.normal(k1, (B, N, C), dtype=jnp.float32)
        w_qkv = jax.random.normal(k2, (3 * C, C), dtype=jnp.float32) * C ** (-0.5)
        w_proj = jax.random.normal(k3, (C, C), dtype=jnp.float32) * C ** (-0.5)
        return {'x': x, 'w_qkv': w_qkv, 'w_proj': w_proj}
    _L0_attn_in = _L0_attn_setup()

    def _L0_ffn_setup():
        import jax, jax.numpy as jnp
        import numpy as np
        B, M, D = (4, 256, 128)
        N, P = (64, 32)
        key = jax.random.key(seed)
        k1, k2, k3, k4 = jax.random.split(key, 4)
        x = jax.random.normal(k1, (B, M, D), dtype=jnp.float32)
        phi = jax.random.normal(k2, (D, N, P), dtype=jnp.float32) * (1.0 / np.sqrt(D))
        W = jax.random.normal(k3, (N, D, D), dtype=jnp.float32) * (1.0 / np.sqrt(D))
        b = jax.random.normal(k4, (N, D), dtype=jnp.float32) * 0.01
        return {'x': x, 'phi': phi, 'W': W, 'b': b}
    _L0_ffn_in = _L0_ffn_setup()
    _d = {'L0_attn_x': _L0_attn_in['x'], 'L0_attn_w_qkv': _L0_attn_in['w_qkv'], 'L0_attn_w_proj': _L0_attn_in['w_proj'], 'L0_ffn_phi': _L0_ffn_in['phi'], 'L0_ffn_W': _L0_ffn_in['W'], 'L0_ffn_b': _L0_ffn_in['b']}
    _x0 = _d['L0_attn_x']
    _d['L0_attn_x'] = jax.random.normal(jax.random.fold_in(jax.random.key(seed), 1), (8, 512, 128), dtype=_x0.dtype)
    del _x0
    return _d

def reference(L0_attn_x, L0_attn_w_qkv, L0_attn_w_proj, L0_ffn_phi, L0_ffn_W, L0_ffn_b):

    def _L0_attn_ref(x, w_qkv, w_proj):
        import jax, jax.numpy as jnp
        import numpy as np
        H = 16
        RMS_EPS = 1.1920928955078125e-07
        NORM_EPS = 1e-12

        def _rms_norm(t):
            ms = jnp.mean(t * t, axis=-1, keepdims=True)
            return t * jax.lax.rsqrt(ms + RMS_EPS)
        B, N, C = x.shape
        D = C // H
        scale = D ** (-0.5)
        qkv = x @ w_qkv.T
        qkv = qkv.reshape(B, N, 3, H, D)
        q = qkv[:, :, 0].transpose(0, 2, 1, 3)
        k = qkv[:, :, 1].transpose(0, 2, 1, 3)
        v = qkv[:, :, 2].transpose(0, 2, 1, 3)
        q = _rms_norm(q)
        k = _rms_norm(k)
        attn = jnp.einsum('bhnd,bhmd->bhnm', q, k) * scale
        attn = jax.nn.softmax(attn, axis=-1)
        y = jnp.einsum('bhnm,bhmd->bhnd', attn, v)
        vnorm = jnp.linalg.norm(v, axis=-1, keepdims=True)
        Vn = v / jnp.maximum(vnorm, NORM_EPS)
        y = y - jnp.sum(y * Vn, axis=-1, keepdims=True) * Vn
        out = y.transpose(0, 2, 1, 3).reshape(B, N, C)
        return out @ w_proj.T

    def _L0_ffn_ref(x, phi, W, b):
        import jax, jax.numpy as jnp
        import numpy as np
        B, M, D = (4, 256, 128)
        N, P = (64, 32)
        logits = jnp.einsum('bmd,dnp->bmnp', x, phi)
        dispatch = jax.nn.softmax(logits, axis=0)
        bsz, m, n, p = logits.shape
        combine = jax.nn.softmax(logits.reshape(bsz, m, n * p), axis=-1).reshape(bsz, m, n, p)
        slots = jnp.einsum('bmd,bmnp->bnpd', x, dispatch)
        y = jnp.einsum('bnpd,nde->bnpe', slots, W) + b[None, :, None, :]
        out = jnp.einsum('bnpd,bmnp->bmd', y, combine)
        return out
    x = L0_attn_x
    xn = _layernorm(x, axis=-1)
    x = x + _L0_attn_ref(xn, L0_attn_w_qkv, L0_attn_w_proj) + _L0_ffn_ref(xn, L0_ffn_phi, L0_ffn_W, L0_ffn_b)
    return x

_drawn_inputs = setup_inputs


def setup_inputs(seed=0):
    import zlib

    import numpy as np

    out = dict(_drawn_inputs(seed))
    spreads = {}
    factors = {'L0_ffn_b': 45.998}
    for name, (base, spread) in spreads.items():
        noise = np.random.default_rng([zlib.crc32(name.encode()), seed]).standard_normal(out[name].shape)
        drawn = base * np.exp(spread * noise) if base else spread * noise
        out[name] = jnp.asarray(drawn.astype(out[name].dtype))
    for name, factor in factors.items():
        out[name] = (out[name] * factor).astype(out[name].dtype)
    return out
```

```python
from contextlib import ExitStack

import concourse.bass as bass
from concourse import mybir

F32 = mybir.dt.float32
F32R = mybir.dt.float32r
F16 = mybir.dt.float16
BF16 = mybir.dt.bfloat16
ALU = mybir.AluOpType
ACT = mybir.ActivationFunctionType
AX = mybir.AxisListType

P = 128
NB, NT, C = 8, 512, 128
H, DH = 16, 8
NE, NP = 64, 32
S = NE * NP
TT = NT // P
SW = 256
NS = S // SW
SUB = SW // P
EC = SW // NP
HG = 4
NHG = H // HG
PAD = 32
VC = DH + 1
VW = (H - 1) * VC + PAD + 1
NU = NHG * TT
RMS_EPS = 1.1920928955078125e-07
LN_EPS = 1e-5
NORM_EPS2 = 1e-24
SCALE = DH ** -0.5
assert NU == NB * SUB and NS == NB and EC * NE // EC == NE


class Signal:

    def __init__(self, ctx, nc, name, per, first=0, by=1):
        self.sem = ctx.enter_context(nc.semaphore(name))
        self.per, self.first, self.by = per, first, by

    def at(self, k, n):
        return (k - self.first) * (self.per * self.by) + n * self.by


def later(k):
    return not isinstance(k, int) or k > 0


def program(nc, x, w_qkv, w_proj, phi, W, b, out):
    ctx = ExitStack()
    with ctx:
        def sb(name, shape, dt=F32):
            return ctx.enter_context(nc.sbuf_tensor(name, shape, dt))

        def sig(name, per, first=0, by=1):
            return Signal(ctx, nc, name, per, first, by)

        xn = sb("xn", [P, NB * TT, C])
        xnT_h = sb("xnT_h", [P, NB * NT], F32R)
        xnT_l = sb("xnT_l", [P, NB * NT], F32R)
        D = sb("D", [P, TT, NB, SW])
        acc = sb("acc", [P, NB, TT, C])
        phi_raw = sb("phi_raw", [P, SW])
        phi1_h, phi1_l = sb("phi1_h", [P, SW], F32R), sb("phi1_l", [P, SW], F32R)
        phi2_h, phi2_l = sb("phi2_h", [P, SW], F32R), sb("phi2_l", [P, SW], F32R)
        W_sb = sb("W_sb", [P, EC, C])
        bias_sb = sb("bias_sb", [P, SUB, C])
        slots_sb = sb("slots_sb", [P, 2, 2, SW])
        y = sb("y", [P, NB, SUB, C])
        E2 = sb("E2", [P, 4, NT])
        oT_sb = sb("oT_sb", [P, 2, NT])
        o_scaled = sb("o_scaled", [P, TT, C])
        batch_max = sb("batch_max", [P, 2, SW])
        batch_sum = sb("batch_sum", [P, 2, SW])
        row_max = sb("row_max", [P, TT, NB])
        neg_max = sb("neg_max", [P, TT, NB])
        neg_rest = sb("neg_rest", [P, 2, TT, NB])
        neg_parts = sb("neg_parts", [P, TT, 3, NB], BF16)
        negT = sb("negT", [TT * 3 * NB, P], BF16)
        neg_rows = sb("neg_rows", [3 * NB, NT], BF16)
        pick = sb("pick", [3 * NB, NB, P], BF16)
        dump = sb("dump", [P, 4, SW], BF16)
        Z = sb("Z", [P, TT, NB])
        Zs = sb("Zs", [P, TT, NB])
        Z_run = sb("Z_run", [P, TT, NB])
        m_run = sb("m_run", [P, TT, NB])
        m_new = sb("m_new", [P, TT, NB])
        ab_log = sb("ab_log", [P, 2, TT, NB])
        ab = sb("ab", [P, 2, TT, NB])
        ident = sb("ident", [P, P])
        ident16 = sb("ident16", [P, P], F16)
        identb = sb("identb", [P, P], BF16)
        minus_half = sb("minus_half", [P, P])
        wq_h, wq_l = sb("wq_h", [P, 3 * C], F32R), sb("wq_l", [P, 3 * C], F32R)
        wp = sb("wp", [P, C])
        xb_h, xb_l = sb("xb_h", [P, NT], F32R), sb("xb_l", [P, NT], F32R)
        qkv = sb("qkv", [P, TT, 3 * C])
        work = sb("work", [P, 2, TT, C])
        mean_sq = sb("mean_sq", [P, P])
        rms = sb("rms", [P, P])
        stack = sb("stack", [P, 2, TT * H, 4, DH], F16)
        stackT = sb("stackT", [P, 2, NHG, NT], F16)
        V1 = sb("V1", [P, TT, VW])
        probs = sb("probs", [P, 4, 2, NT])
        yT_sb = sb("yT_sb", [P, 2, NT])
        Y = sb("Y", [P, TT, H, VC])
        vv = sb("vv", [P, TT * H])
        dots = sb("dots", [P, TT * H])
        inv_den = sb("inv_den", [P, TT * H])
        AO = work[:, 0]
        AOT = yT_sb[:, 0]
        x_attn = sb("x_attn", [P, TT, C])
        ln_sum = sb("ln_sum", [P, NB, TT])
        ln_mean = sb("ln_mean", [P, NB, TT])
        ln_var = sb("ln_var", [P, NB, TT])
        ln_rstd = sb("ln_rstd", [P, NB, TT])

        def bank(name):
            return ctx.enter_context(nc.psum_tensor(name, [P, 512], F32))

        sc = ctx.enter_context(nc.psum_tensor("sc", [P, 2, 512], F32))
        pvb = bank("pvb")
        L = [bank("L0"), bank("L1")]
        Fb = bank("Fb")
        M0 = bank("M0")
        M1 = bank("M1")

        x_in = [sig(f"x_in{n}", 1, by=16) for n in range(NB)]
        w_in = sig("w_in", 2, by=16)
        phi_in = sig("phi_in", 1, by=16)
        W_in = sig("W_in", 1, by=16)
        bias_in = sig("bias_in", SUB, by=16)
        xb_in = sig("xb_in", 2, by=16)
        xa_in = sig("xa_in", 1, by=16)
        neg_in = sig("neg_in", TT, by=16)
        xa_out = sig("xa_out", 1, by=16)
        xa_back = sig("xa_back", 1, by=16)
        stored = sig("stored", NB, by=16)
        consts, picks = sig("consts", 12), sig("picks", 3)
        p_sum, p_mean, p_cent = sig("p_sum", NB), sig("p_mean", NB), sig("p_cent", NB)
        p_sq, p_var, p_eps = sig("p_sq", NB), sig("p_var", NB), sig("p_eps", NB)
        p_rstd, p_xn = sig("p_rstd", NB), sig("p_xn", NB)
        p_T, p_Th, p_Tl = sig("p_T", NB), sig("p_Th", NB), sig("p_Tl", NB)
        p_wT, p_wh, p_wl = sig("p_wT", 2), sig("p_wh", 2), sig("p_wl", 1)
        qkv_ready, logits_ready, stackT_ready = sig("qkv_ready", TT), sig("logits_ready", NU), sig("stackT_ready", 4)
        scores_ready, pv_done, yT_ready = sig("scores_ready", 2 * NU), sig("pv_done", NU), sig("yT_ready", NHG)
        lgT_ready, o_done, oT_ready = sig("lgT_ready", NU, 1), sig("o_done", NU, 1), sig("oT_ready", NB, 1)
        negT_ready, slots_ready, y_ready = sig("negT_ready", 1), sig("slots_ready", 4), sig("y_ready", 4)
        aoT_ready, proj_ready = sig("aoT_ready", 1), sig("proj_ready", 1)
        qkv_out, D_out, V_out = sig("qkv_out", TT), sig("D_out", NU), sig("V_out", 1)
        probs_out, Z_out, E_out = sig("probs_out", 2 * NU), sig("Z_out", TT * NB), sig("E_out", TT)
        E2_out, oT_out, yT_out = sig("E2_out", NU, 1), sig("oT_out", NB, 1), sig("yT_out", NHG)
        slots_out, AOT_out, ab_out = sig("slots_out", 4), sig("AOT_out", 1), sig("ab_out", 1)
        phi2_out, phi1h_out, phi1_out = sig("phi2_out", 2, 1), sig("phi1h_out", 1), sig("phi1_out", 1)
        sq_out, ms_out, half_out, stack_out = sig("sq_out", 1), sig("ms_out", 2), sig("half_out", 2), sig("stack_out", 2)
        rmax_out, bmax_out, nmax_out = sig("rmax_out", TT), sig("bmax_out", TT), sig("nmax_out", TT)
        parts_out, negT_out = sig("parts_out", 5), sig("negT_out", 1)
        bsum_out, brec_out = sig("bsum_out", TT), sig("brec_out", TT)
        stackT_out, Y_out, scaled_out = sig("stackT_out", 4), sig("Y_out", NHG), sig("scaled_out", NB, 1)
        vv_out, post_out, AO_out = sig("vv_out", 3), sig("post_out", 6), sig("AO_out", 1)
        y_out, xa_sum, flash_out = sig("y_out", 4), sig("xa_sum", 1), sig("flash_out", 4)
        fin_rz, fin_mul = sig("fin_rz", 1), sig("fin_mul", NB)
        rms_out, normed_out, vsq_out = sig("rms_out", 1), sig("normed_out", 2), sig("vsq_out", 1)
        sub_out, disp_out = sig("sub_out", TT), sig("disp_out", TT)
        accA_out, accB_out, Zrun_out = sig("accA_out", NB, 1), sig("accB_out", NB, 1), sig("Zrun_out", 3)
        fin_add = sig("fin_add", NB)

        x_stage = D[:, 0:2].rearrange("p a b s -> p (a b s)").rearrange("p (b t c) -> p b t c", b=NB, t=TT)
        w_stage = probs[:, 0, 0, 0:3 * C].rearrange("p (r c) -> p r c", r=3)
        wp_stage = probs[:, 0, 1, 0:C]
        ln_sq = acc
        x_tiles = x.rearrange("b (t p) c -> p b t c", p=P)
        out_tiles = out.rearrange("b (t p) c -> p b t c", p=P)
        phi_v = phi.rearrange("d n s -> d (n s)")
        W_v = W.rearrange("n d e -> d n e")
        V_v = qkv[:, :, 2 * C:3 * C].rearrange("p t (h d) -> p t h d", h=H)

        def per_head(t):
            return t.rearrange("p (t h) -> p t h", t=TT).unsqueeze(3).to_broadcast([P, TT, H, DH])

        block = ctx.enter_context(nc.Block())

        @block.sync
        def _(sp):
            def load_phi(k):
                if later(k):
                    sp.wait_ge(phi1_out.sem, phi1_out.at(k - 1, 1))
                sp.dma_start(phi_raw[:], phi_v[:, bass.ds(k * SW, SW)]).then_inc(phi_in.sem, 16)

            def load_xb(k):
                if later(k):
                    sp.wait_ge(qkv_ready.sem, qkv_ready.at(k - 1, TT))
                for dst, src in ((xb_h, xnT_h), (xb_l, xnT_l)):
                    sp.dma_start(dst[:].bitcast(F32), src[:, bass.ds(k * NT, NT)].bitcast(F32)).then_inc(xb_in.sem, 16)

            def stage(k, ahead):
                if later(k):
                    sp.wait_ge(y_ready.sem, y_ready.at(k - 1, 4))
                sp.dma_start(W_sb[:], W_v[:, bass.ds(k * EC, EC), :]).then_inc(W_in.sem, 16)
                if later(k):
                    sp.wait_ge(y_out.sem, y_out.at(k - 1, 4))
                for u in range(SUB):
                    rows = b[bass.ds(k * EC + u * (P // NP), P // NP), :]
                    sp.dma_start(bias_sb[:, u, :], rows.unsqueeze(1).to_broadcast([P // NP, NP, C])).then_inc(bias_in.sem, 16)
                if later(k):
                    sp.wait_ge(xa_out.sem, xa_out.at(k - 1, 1))
                sp.dma_start(x_attn[:], tiles_of(x, k)).then_inc(xa_in.sem, 16)
                if ahead:
                    load_phi(k + 1)
                    load_xb(k + 1)
                sp.wait_ge(negT_out.sem, negT_out.at(k, 1))
                if not isinstance(k, int) or k > 0:
                    sp.wait_ge(lgT_ready.sem, lgT_ready.at(k, NU))
                for t in range(TT):
                    rows = 3 * NB
                    sp.dma_start(neg_rows[:, t * P:(t + 1) * P], negT[t * rows:(t + 1) * rows, :]).then_inc(neg_in.sem, 16)
                sp.wait_ge(xa_sum.sem, xa_sum.at(k, 1))
                sp.dma_start(tiles_of(out, k), x_attn[:]).then_inc(xa_out.sem, 16)

            def tiles_of(t, k):
                return t[bass.ds(k, 1)].rearrange("b (t p) c -> p (b t) c", p=P)

            sp.dma_start(w_stage, w_qkv.rearrange("(r p) c -> p r c", p=P)).then_inc(w_in.sem, 16)
            sp.dma_start(wp_stage, w_proj).then_inc(w_in.sem, 16)
            for n in range(NB):
                sp.dma_start(x_stage[:, n], x_tiles[:, n]).then_inc(x_in[n].sem, 16)
            load_phi(0)
            sp.wait_ge(p_Th.sem, p_Th.at(0, 1))
            sp.wait_ge(p_Tl.sem, p_Tl.at(0, 1))
            load_xb(0)
            sp.wait_ge(p_Tl.sem, p_Tl.at(0, 2))
            stage(0, True)
            with sp.Fori(1, NS - 1) as k:
                stage(k, True)
            stage(NS - 1, False)
            sp.wait_ge(slots_ready.sem, slots_ready.at(NS - 1, 4))
            sp.wait_ge(xa_out.sem, xa_out.at(NS - 1, 1))
            sp.dma_start(x_stage, out_tiles).then_inc(xa_back.sem, 16)
            for n in range(NB):
                sp.wait_ge(fin_add.sem, fin_add.at(0, n + 1))
                sp.dma_start(out_tiles[:, n], acc[:, n]).then_inc(stored.sem, 16)
            sp.wait_ge(stored.sem, NB * 16)

        @block.tensor
        def _(pe):
            def halves(dst, parts, start=True, stop=True):
                for n, (st, mv) in enumerate(parts):
                    last = nc.tensor.matmul(dst, st, mv, start=start and n == 0, stop=stop and n == len(parts) - 1)
                return last

            def qkv_products(k):
                pe.wait_ge(xb_in.sem, xb_in.at(k, 2))
                for t in range(TT):
                    if t == 0 and later(k):
                        pe.wait_ge(xa_sum.sem, xa_sum.at(k - 1, 1))
                    if t > 0:
                        pe.wait_ge(qkv_out.sem, qkv_out.at(k, t))
                    h, l = xb_h[:, t * P:(t + 1) * P], xb_l[:, t * P:(t + 1) * P]
                    halves(M0[:, 0:3 * C], ((h, wq_h[:]), (h, wq_l[:]), (l, wq_h[:]))).then_inc(qkv_ready.sem, 1)

            def logits(k):
                pe.wait_ge(phi1_out.sem, phi1_out.at(k, 1))
                for i in range(NU):
                    t, pr = divmod(i, NB // 2)
                    if i >= 2:
                        pe.wait_ge(D_out.sem, D_out.at(k, i - 1))
                    for n in range(2):
                        at = (2 * pr + n) * NT + t * P
                        h, l = xnT_h[:, at:at + P], xnT_l[:, at:at + P]
                        last = halves(L[i % 2][:, n * SW:(n + 1) * SW],
                                      ((h, phi1_h[:]), (h, phi1_l[:]), (l, phi1_h[:])))
                    last.then_inc(logits_ready.sem, 1)

            def stack_transposes(k):
                out16 = M0[:].bitcast(F16)
                for g in range(4):
                    which, pair = divmod(g, 2)
                    if g == 0:
                        pe.wait_ge(qkv_out.sem, qkv_out.at(k, TT))
                    pe.wait_ge(stack_out.sem, stack_out.at(k, which + 1))
                    if g > 0:
                        pe.wait_ge(stackT_out.sem, stackT_out.at(k, g))
                    for n in range(2):
                        for t in range(TT):
                            at = t * H + (2 * pair + n) * HG
                            last = nc.tensor.transpose(
                                out16[:, (n * TT + t) * P:(n * TT + t + 1) * P],
                                stack[:, which, at:at + HG].rearrange("p h f d -> p (h f d)"), ident16[:])
                    last.then_inc(stackT_ready.sem, 1)

            def scores(k, pair):
                u, half = divmod(pair, 2)
                hg, kt = divmod(u, TT)
                if pair > 0:
                    pe.wait_ge(probs_out.sem, probs_out.at(k, pair))
                for n in range(2):
                    r = PAD * (2 * half + n)
                    last = nc.tensor.matmul(sc[:, n, :], stackT[r:r + PAD, 1, hg, kt * P:(kt + 1) * P],
                                            stackT[r:r + PAD, 0, hg, :], start=True, stop=True)
                last.then_inc(scores_ready.sem, 1)

            def pv(k, u):
                hg, kt = divmod(u, TT)
                pe.wait_ge(probs_out.sem, probs_out.at(k, 2 * u + 2))
                if u == 0:
                    pe.wait_ge(V_out.sem, V_out.at(k, 1))
                if kt == 0 and hg > 0:
                    pe.wait_ge(yT_out.sem, yT_out.at(k, hg))
                for j in range(HG):
                    at = (hg * HG + j) * VC
                    last = nc.tensor.matmul(pvb[PAD * j:PAD * (j + 1), :], V1[:, kt, at:at + PAD],
                                            probs[:, (2 * u + j // 2) % 4, j % 2, :],
                                            start=kt == 0, stop=kt == TT - 1)
                last.then_inc(pv_done.sem, 1)

            def yT_back(k, hg):
                pe.wait_ge(yT_out.sem, yT_out.at(k, hg + 1))
                if hg > 0:
                    pe.wait_ge(Y_out.sem, Y_out.at(k, hg))
                for t in range(TT):
                    last = nc.tensor.transpose(M0[:, t * P:(t + 1) * P], yT_sb[:, hg % 2, t * P:(t + 1) * P], ident[:])
                last.then_inc(yT_ready.sem, 1)

            def logits_T(k, v):
                n, u = divmod(v, SUB)
                if v == 0:
                    pe.wait_ge(phi2_out.sem, phi2_out.at(k, 2))
                    pe.wait_ge(neg_in.sem, neg_in.at(k - 1, TT))
                    pe.wait_ge(y_out.sem, y_out.at(k - 1, 4))
                else:
                    pe.wait_ge(E2_out.sem, E2_out.at(k, v))
                s, m = slice(u * P, (u + 1) * P), slice(n * NT, (n + 1) * NT)
                halves(Fb[:], ((phi2_h[:, s], xnT_h[:, m]), (phi2_h[:, s], xnT_l[:, m]),
                               (phi2_l[:, s], xnT_h[:, m]), (pick[:, n, :], neg_rows[:]))).then_inc(lgT_ready.sem, 1)

            def combine(k, v, attn):
                n, u = divmod(v, SUB)
                pe.wait_ge(E2_out.sem, E2_out.at(k, v + 1))
                if n < 2 and u == 0 and attn:
                    pe.wait_ge(D_out.sem, D_out.at(k, NU))
                if n >= 2 and u == 0:
                    pe.wait_ge(oT_out.sem, oT_out.at(k, n - 1))
                nc.tensor.matmul(L[n % 2][:], y[:, n, u, :], E2[:, v % 4, :],
                                 start=u == 0, stop=u == SUB - 1).then_inc(o_done.sem, 1)

            def oT_back(k, n, attn):
                pe.wait_ge(oT_out.sem, oT_out.at(k, n + 1))
                if n == 1 and attn:
                    pe.wait_ge(negT_out.sem, negT_out.at(k, 1))
                if n >= 1:
                    pe.wait_ge(scaled_out.sem, scaled_out.at(k, n))
                for t in range(TT):
                    last = nc.tensor.transpose(M1[:, t * P:(t + 1) * P], oT_sb[:, n % 2, t * P:(t + 1) * P], ident[:])
                last.then_inc(oT_ready.sem, 1)

            def neg_transpose(k, ffn2):
                pe.wait_ge(parts_out.sem, parts_out.at(k, 5))
                if ffn2:
                    pe.wait_ge(scaled_out.sem, scaled_out.at(k, 1))
                nc.tensor.transpose(M1[:].bitcast(BF16)[0:TT * 3 * NB, 0:P],
                                    neg_parts[:].rearrange("p t a b -> p (t a b)"), identb[:]).then_inc(negT_ready.sem, 1)

            def slots(k, pr, ffn2):
                if pr == 0:
                    pe.wait_ge(disp_out.sem, disp_out.at(k, TT))
                if pr < 2 and ffn2:
                    pe.wait_ge(oT_out.sem, oT_out.at(k, NB - 1 + pr))
                if pr < 2:
                    pe.wait_ge(D_out.sem, D_out.at(k, NU))
                else:
                    pe.wait_ge(slots_out.sem, slots_out.at(k, pr - 1))
                for n in range(2):
                    for t in range(TT):
                        last = nc.tensor.matmul(L[pr % 2][:, n * SW:(n + 1) * SW], xn[:, (2 * pr + n) * TT + t, :],
                                                D[:, t, 2 * pr + n, :], start=t == 0, stop=t == TT - 1)
                last.then_inc(slots_ready.sem, 1)

            def experts(k, pr):
                pe.wait_ge(slots_out.sem, slots_out.at(k, pr + 1))
                if pr == 0:
                    pe.wait_ge(W_in.sem, W_in.at(k, 1))
                    pe.wait_ge(probs_out.sem, probs_out.at(k, 2 * NU))
                if pr >= 2:
                    pe.wait_ge(y_out.sem, y_out.at(k, pr - 1))
                for n in range(2):
                    for u in range(SUB):
                        for j in range(P // NP):
                            at = u * P + j * NP
                            last = nc.tensor.matmul(
                                sc[j * NP:(j + 1) * NP, pr % 2, (n * SUB + u) * C:(n * SUB + u + 1) * C],
                                slots_sb[:, pr % 2, n, at:at + NP], W_sb[:, u * (P // NP) + j, :], start=True, stop=True)
                last.then_inc(y_ready.sem, 1)

            def project(k):
                pe.wait_ge(AO_out.sem, AO_out.at(k, 1))
                for t in range(TT):
                    last = nc.tensor.transpose(M0[:, t * P:(t + 1) * P], AO[:, t, :], ident[:])
                last.then_inc(aoT_ready.sem, 1)
                pe.wait_ge(AOT_out.sem, AOT_out.at(k, 1))
                for t in range(TT):
                    last = nc.tensor.matmul(M0[:, t * C:(t + 1) * C], AOT[:, t * P:(t + 1) * P], wp[:], start=True, stop=True)
                last.then_inc(proj_ready.sem, 1)

            def stage(k, ffn2):
                qkv_products(k)
                logits(k)
                stack_transposes(k)
                pe.wait_ge(stackT_out.sem, stackT_out.at(k, 4))
                if later(k):
                    pe.wait_ge(y_out.sem, y_out.at(k - 1, 4))
                for u in range(NU):
                    scores(k, 2 * u)
                    if ffn2:
                        logits_T(k, u)
                        if u > 0:
                            combine(k, u - 1, True)
                    scores(k, 2 * u + 1)
                    if u > 0:
                        pv(k, u - 1)
                    if ffn2 and u % 2 == 1 and u >= 3:
                        oT_back(k, (u - 3) // 2, True)
                    if u == 4:
                        neg_transpose(k, ffn2)
                    if u % TT == 1 and u > TT:
                        yT_back(k, u // TT - 1)
                if ffn2:
                    combine(k, NU - 1, True)
                pv(k, NU - 1)
                slots(k, 0, ffn2)
                yT_back(k, NHG - 1)
                if ffn2:
                    oT_back(k, NB - 1, True)
                slots(k, 1, ffn2)
                experts(k, 0)
                slots(k, 2, ffn2)
                experts(k, 1)
                slots(k, 3, ffn2)
                experts(k, 2)
                experts(k, 3)
                project(k)

            pe.wait_ge(consts.sem, consts.at(0, 4))
            pe.wait_ge(w_in.sem, w_in.at(0, 2))
            for r in range(3):
                last = nc.tensor.transpose(M0[:, r * P:(r + 1) * P], w_stage[:, r, :], ident[:])
            last.then_inc(p_wT.sem, 1)
            nc.tensor.transpose(M1[:, 0:P], wp_stage, ident[:]).then_inc(p_wT.sem, 1)
            for n in range(NB):
                pe.wait_ge(p_xn.sem, p_xn.at(0, n + 1))
                if n >= 2:
                    pe.wait_ge(p_Tl.sem, p_Tl.at(0, n - 1))
                for t in range(TT):
                    last = nc.tensor.transpose(L[n % 2][:, t * P:(t + 1) * P], xn[:, n * TT + t, :], ident[:])
                last.then_inc(p_T.sem, 1)
            pe.wait_ge(consts.sem, consts.at(0, 12))
            pe.wait_ge(p_wh.sem, p_wh.at(0, 2))
            pe.wait_ge(p_wl.sem, p_wl.at(0, 1))
            pe.wait_ge(p_Tl.sem, p_Tl.at(0, NB))
            stage(0, False)
            with pe.Fori(1, NS) as k:
                stage(k, True)
            for v in range(NU):
                logits_T(NS, v)
                if v > 0:
                    combine(NS, v - 1, False)
                if v % 2 == 1 and v >= 3:
                    oT_back(NS, (v - 3) // 2, False)
            combine(NS, NU - 1, False)
            oT_back(NS, NB - 1, False)

        @block.scalar
        def _(act):
            def copy(dst, src):
                return nc.scalar.activation(dst, src, ACT.Copy)

            def row_sums(k, t):
                act.wait_ge(nmax_out.sem, nmax_out.at(k, t + 1))
                if t == 0:
                    if later(k):
                        act.wait_ge(Zrun_out.sem, Zrun_out.at(k - 1, 3))
                for n in range(NB):
                    at = t * NB + n
                    if at >= 4:
                        act.wait_ge(Z_out.sem, Z_out.at(k, at - 3))
                    nc.scalar.activation(dump[:, n % 4, :], D[:, t, n, :], ACT.Exp, bias=neg_max[:, t, n:n + 1],
                                         accum_out=Z[:, t, n:n + 1]).then_inc(Z_out.sem, 1)

            def dispatch_exp(k, t):
                act.wait_ge(sub_out.sem, sub_out.at(k, t + 1))
                nc.scalar.activation(D[:, t], D[:, t], ACT.Exp).then_inc(E_out.sem, 1)

            def probabilities(k, pair):
                act.wait_ge(scores_ready.sem, scores_ready.at(k, pair + 1))
                if pair >= 4:
                    act.wait_ge(pv_done.sem, pv_done.at(k, pair // 2 - 1))
                nc.scalar.activation(probs[:, pair % 4], sc[:], ACT.Exp, scale=SCALE).then_inc(probs_out.sem, 1)

            def combine_exp(k, v):
                act.wait_ge(lgT_ready.sem, lgT_ready.at(k, v + 1))
                if v >= 4:
                    act.wait_ge(o_done.sem, o_done.at(k, v - 3))
                nc.scalar.activation(E2[:, v % 4, :], Fb[:], ACT.Exp).then_inc(E2_out.sem, 1)

            def oT_copy(k, n):
                act.wait_ge(o_done.sem, o_done.at(k, SUB * (n + 1)))
                if n >= 2:
                    act.wait_ge(oT_ready.sem, oT_ready.at(k, n - 1))
                copy(oT_sb[:, n % 2, :], L[n % 2][:]).then_inc(oT_out.sem, 1)

            def yT_copy(k, hg):
                act.wait_ge(pv_done.sem, pv_done.at(k, TT * (hg + 1)))
                if hg >= 2:
                    act.wait_ge(yT_ready.sem, yT_ready.at(k, hg - 1))
                copy(yT_sb[:, hg % 2, :], pvb[:]).then_inc(yT_out.sem, 1)

            def stage(k, ffn2):
                if later(k):
                    act.wait_ge(AO_out.sem, AO_out.at(k - 1, 1))
                for t in range(TT):
                    act.wait_ge(qkv_ready.sem, qkv_ready.at(k, t + 1))
                    copy(qkv[:, t, :], M0[:, 0:3 * C]).then_inc(qkv_out.sem, 1)
                act.wait_ge(qkv_out.sem, qkv_out.at(k, TT))
                copy(V1[:, :, 0:H * VC].rearrange("p t (h d) -> p t h d", h=H)[:, :, :, 0:DH], V_v).then_inc(V_out.sem, 1)
                for i in range(NU):
                    t, pr = divmod(i, NB // 2)
                    act.wait_ge(logits_ready.sem, logits_ready.at(k, i + 1))
                    copy(D[:, t, 2 * pr:2 * pr + 2, :].rearrange("p b s -> p (b s)"), L[i % 2][:]).then_inc(D_out.sem, 1)
                row_sums(k, 0)
                for u in range(NU):
                    probabilities(k, 2 * u)
                    if ffn2:
                        combine_exp(k, u)
                    if u < 3:
                        row_sums(k, u + 1)
                    probabilities(k, 2 * u + 1)
                    if ffn2 and u % 2 == 0 and u >= 2:
                        oT_copy(k, (u - 2) // 2)
                    if u % TT == 0 and u >= TT:
                        yT_copy(k, u // TT - 1)
                    if u in (3, 5, 7, 9):
                        dispatch_exp(k, (u - 3) // 2)
                if ffn2:
                    oT_copy(k, NB - 1)
                yT_copy(k, NHG - 1)
                for pr in range(4):
                    act.wait_ge(slots_ready.sem, slots_ready.at(k, pr + 1))
                    if pr >= 2:
                        act.wait_ge(y_ready.sem, y_ready.at(k, pr - 1))
                    copy(slots_sb[:, pr % 2].rearrange("p n s -> p (n s)"), L[pr % 2][:]).then_inc(slots_out.sem, 1)
                act.wait_ge(aoT_ready.sem, aoT_ready.at(k, 1))
                copy(AOT, M0[:]).then_inc(AOT_out.sem, 1)
                act.wait_ge(flash_out.sem, flash_out.at(k, 4))
                if ffn2:
                    act.wait_ge(accB_out.sem, accB_out.at(k, NB))
                nc.scalar.activation(ab[:], ab_log[:], ACT.Exp).then_inc(ab_out.sem, 1)

            act.wait_ge(p_wT.sem, p_wT.at(0, 1))
            copy(wq_h[:], M0[:, 0:3 * C]).then_inc(p_wh.sem, 1)
            act.wait_ge(p_wT.sem, p_wT.at(0, 2))
            copy(wp[:], M1[:, 0:C]).then_inc(p_wh.sem, 1)
            for n in range(NB):
                act.wait_ge(p_T.sem, p_T.at(0, n + 1))
                copy(xnT_h[:, n * NT:(n + 1) * NT], L[n % 2][:]).then_inc(p_Th.sem, 1)
            act.wait_ge(consts.sem, consts.at(0, 12))
            act.wait_ge(p_xn.sem, p_xn.at(0, NB))
            stage(0, False)
            with act.Fori(1, NS) as k:
                stage(k, True)
            for v in range(NU):
                combine_exp(NS, v)
                if v % 2 == 0 and v >= 2:
                    oT_copy(NS, (v - 2) // 2)
            oT_copy(NS, NB - 1)

        @block.vector
        def _(dve):
            def keep_phi(k):
                dve.wait_ge(y_ready.sem, y_ready.at(k - 1, 4))
                nc.vector.tensor_copy(phi2_h[:], phi1_h[:].bitcast(F32)).then_inc(phi2_out.sem, 1)
                nc.vector.tensor_copy(phi2_l[:], phi1_l[:].bitcast(F32)).then_inc(phi2_out.sem, 1)

            def split_phi(k):
                dve.wait_ge(phi_in.sem, phi_in.at(k, 1))
                nc.vector.tensor_copy(phi1_h[:], phi_raw[:]).then_inc(phi1h_out.sem, 1)
                dve.wait_ge(phi1h_out.sem, phi1h_out.at(k, 1))
                nc.vector.tensor_tensor(phi1_l[:], phi_raw[:], phi1_h[:].bitcast(F32), ALU.subtract).then_inc(phi1_out.sem, 1)

            def mean_squares(k):
                dve.wait_ge(qkv_out.sem, qkv_out.at(k, TT))
                qk = qkv[:, :, 0:2 * C]
                sq = work[:].rearrange("p a t c -> p (a t c)").rearrange("p (t c) -> p t c", t=TT)
                nc.vector.tensor_tensor(sq, qk, qk, ALU.mult).then_inc(sq_out.sem, 1)
                dve.wait_ge(sq_out.sem, sq_out.at(k, 1))
                nc.vector.tensor_reduce(mean_sq[:], work[:].rearrange("p a t c -> p (a t c)").rearrange(
                    "p (g d) -> p g d", d=DH), axis=AX.X, op=ALU.add).then_inc(ms_out.sem, 1)
                dve.wait_ge(ms_out.sem, ms_out.at(k, 1))
                nc.vector.tensor_scalar(mean_sq[:], mean_sq[:], 1.0 / DH, RMS_EPS, ALU.mult, ALU.add).then_inc(ms_out.sem, 1)

            def split_stack(k, which):
                dve.wait_ge(normed_out.sem, normed_out.at(k, which + 1))
                src = work[:, which].rearrange("p t (h d) -> p (t h) d", d=DH).unsqueeze(2).to_broadcast([P, TT * H, 2, DH])
                hi = stack[:, which, :, 0:2, :] if which == 0 else stack[:, which, :, 0:4:2, :]
                lo = stack[:, which, :, 2:4, :] if which == 0 else stack[:, which, :, 1:4:2, :]
                nc.vector.tensor_copy(hi, src).then_inc(half_out.sem, 1)
                dve.wait_ge(half_out.sem, half_out.at(k, which + 1))
                nc.vector.tensor_tensor(lo, src, hi, ALU.subtract).then_inc(stack_out.sem, 1)

            def maxima(k, t):
                dve.wait_ge(D_out.sem, D_out.at(k, 4 * (t + 1)))
                nc.vector.tensor_reduce(row_max[:, t, :], D[:, t], axis=AX.X, op=ALU.max).then_inc(rmax_out.sem, 1)
                if t >= 2:
                    dve.wait_ge(sub_out.sem, sub_out.at(k, t - 1))
                nc.vector.tensor_reduce(batch_max[:, t % 2, :], D[:, t].rearrange("p b s -> p s b"),
                                        axis=AX.X, op=ALU.max).then_inc(bmax_out.sem, 1)
                dve.wait_ge(rmax_out.sem, rmax_out.at(k, t + 1))
                nc.vector.tensor_scalar(neg_max[:, t, :], row_max[:, t, :], -1.0, None, ALU.mult).then_inc(nmax_out.sem, 1)

            def neg_in_parts(k):
                dve.wait_ge(nmax_out.sem, nmax_out.at(k, TT))
                nc.vector.tensor_copy(neg_parts[:, :, 0, :], neg_max[:]).then_inc(parts_out.sem, 1)
                dve.wait_ge(parts_out.sem, parts_out.at(k, 1))
                nc.vector.tensor_tensor(neg_rest[:, 0], neg_max[:], neg_parts[:, :, 0, :], ALU.subtract).then_inc(parts_out.sem, 1)
                dve.wait_ge(parts_out.sem, parts_out.at(k, 2))
                nc.vector.tensor_copy(neg_parts[:, :, 1, :], neg_rest[:, 0]).then_inc(parts_out.sem, 1)
                dve.wait_ge(parts_out.sem, parts_out.at(k, 3))
                nc.vector.tensor_tensor(neg_rest[:, 1], neg_rest[:, 0], neg_parts[:, :, 1, :], ALU.subtract).then_inc(parts_out.sem, 1)
                dve.wait_ge(parts_out.sem, parts_out.at(k, 4))
                nc.vector.tensor_copy(neg_parts[:, :, 2, :], neg_rest[:, 1]).then_inc(parts_out.sem, 1)

            def negT_copy(k):
                dve.wait_ge(negT_ready.sem, negT_ready.at(k, 1))
                if later(k):
                    dve.wait_ge(neg_in.sem, neg_in.at(k - 1, TT))
                nc.vector.tensor_copy(negT[:], M1[:].bitcast(BF16)[0:TT * 3 * NB, 0:P]).then_inc(negT_out.sem, 1)

            def batch_sums(k, t):
                dve.wait_ge(E_out.sem, E_out.at(k, t + 1))
                if t >= 2:
                    dve.wait_ge(disp_out.sem, disp_out.at(k, t - 1))
                nc.vector.tensor_reduce(batch_sum[:, t % 2, :], D[:, t].rearrange("p b s -> p s b"),
                                        axis=AX.X, op=ALU.add).then_inc(bsum_out.sem, 1)
                dve.wait_ge(bsum_out.sem, bsum_out.at(k, t + 1))
                nc.vector.reciprocal(batch_sum[:, t % 2, :], batch_sum[:, t % 2, :]).then_inc(brec_out.sem, 1)

            def scale_out(k, n):
                dve.wait_ge(oT_ready.sem, oT_ready.at(k, n + 1))
                if n == 0:
                    dve.wait_ge(ab_out.sem, ab_out.at(k - 1, 1))
                else:
                    dve.wait_ge(accB_out.sem, accB_out.at(k, n))
                nc.vector.tensor_tensor(o_scaled[:], M1[:].rearrange("p (t c) -> p t c", t=TT),
                                        ab[:, 1, :, n:n + 1].to_broadcast([P, TT, C]), ALU.mult).then_inc(scaled_out.sem, 1)

            def take_Y(k, hg):
                dve.wait_ge(yT_ready.sem, yT_ready.at(k, hg + 1))
                nc.vector.tensor_copy(Y[:, :, hg * HG:(hg + 1) * HG, :],
                                      M0[:].rearrange("p (t j r) -> p t j r", t=TT, j=HG)[:, :, :, 0:VC]).then_inc(Y_out.sem, 1)

            def v_norms(k):
                dve.wait_ge(vsq_out.sem, vsq_out.at(k, 1))
                nc.vector.tensor_reduce(vv[:], work[:, 0].rearrange("p t (h d) -> p (t h) d", d=DH),
                                        axis=AX.X, op=ALU.add).then_inc(vv_out.sem, 1)
                dve.wait_ge(vv_out.sem, vv_out.at(k, 1))
                nc.vector.tensor_scalar(vv[:], vv[:], NORM_EPS2, None, ALU.max).then_inc(vv_out.sem, 1)
                dve.wait_ge(vv_out.sem, vv_out.at(k, 2))
                nc.vector.reciprocal(vv[:], vv[:]).then_inc(vv_out.sem, 1)

            def finish_attention(k):
                w0 = work[:, 0].rearrange("p t (h d) -> p t h d", d=DH)
                w1 = work[:, 1].rearrange("p t (h d) -> p t h d", d=DH)
                dve.wait_ge(Y_out.sem, Y_out.at(k, NHG))
                dve.wait_ge(vv_out.sem, vv_out.at(k, 3))
                nc.vector.tensor_tensor(w1, Y[:, :, :, 0:DH], V_v, ALU.mult).then_inc(post_out.sem, 1)
                nc.vector.reciprocal(inv_den[:].rearrange("p (t h) -> p t h", t=TT), Y[:, :, :, DH]).then_inc(post_out.sem, 1)
                dve.wait_ge(post_out.sem, post_out.at(k, 1))
                nc.vector.tensor_reduce(dots[:], work[:, 1].rearrange("p t (h d) -> p (t h) d", d=DH),
                                        axis=AX.X, op=ALU.add).then_inc(post_out.sem, 1)
                dve.wait_ge(post_out.sem, post_out.at(k, 3))
                nc.vector.tensor_tensor(dots[:], dots[:], vv[:], ALU.mult).then_inc(post_out.sem, 1)
                dve.wait_ge(post_out.sem, post_out.at(k, 4))
                nc.vector.tensor_tensor(w0, V_v, per_head(dots[:]), ALU.mult).then_inc(post_out.sem, 1)
                dve.wait_ge(post_out.sem, post_out.at(k, 5))
                nc.vector.tensor_tensor(w1, Y[:, :, :, 0:DH], w0, ALU.subtract).then_inc(post_out.sem, 1)
                dve.wait_ge(post_out.sem, post_out.at(k, 6))
                nc.vector.tensor_tensor(AO.rearrange("p t (h d) -> p t h d", d=DH), w1, per_head(inv_den[:]),
                                        ALU.mult).then_inc(AO_out.sem, 1)

            def add_bias(k, pr):
                dve.wait_ge(y_ready.sem, y_ready.at(k, pr + 1))
                if pr == 0:
                    dve.wait_ge(bias_in.sem, bias_in.at(k, SUB))
                nc.vector.tensor_tensor(
                    y[:, 2 * pr:2 * pr + 2].rearrange("p n u e -> p n (u e)"),
                    sc[:, pr % 2, :].rearrange("p (n f) -> p n f", n=2),
                    bias_sb[:].rearrange("p u e -> p (u e)").unsqueeze(1).to_broadcast([P, 2, SUB * C]),
                    ALU.add).then_inc(y_out.sem, 1)

            def flash(k):
                nc.vector.tensor_tensor(m_new[:], m_run[:], row_max[:], ALU.max).then_inc(flash_out.sem, 1)
                dve.wait_ge(flash_out.sem, flash_out.at(k, 1))
                nc.vector.tensor_tensor(ab_log[:, 0], m_run[:], m_new[:], ALU.subtract).then_inc(flash_out.sem, 1)
                nc.vector.tensor_tensor(ab_log[:, 1], row_max[:], m_new[:], ALU.subtract).then_inc(flash_out.sem, 1)
                dve.wait_ge(flash_out.sem, flash_out.at(k, 2))
                nc.vector.tensor_copy(m_run[:], m_new[:]).then_inc(flash_out.sem, 1)

            def stage(k, ffn2):
                if ffn2:
                    keep_phi(k)
                    dve.wait_ge(phi2_out.sem, phi2_out.at(k, 2))
                split_phi(k)
                mean_squares(k)
                maxima(k, 0)
                split_stack(k, 0)
                split_stack(k, 1)
                maxima(k, 1)
                for g in range(4):
                    which, pair = divmod(g, 2)
                    dve.wait_ge(stackT_ready.sem, stackT_ready.at(k, g + 1))
                    nc.vector.tensor_copy(stackT[:, which, 2 * pair:2 * pair + 2, :].rearrange("p n m -> p (n m)"),
                                          M0[:].bitcast(F16)).then_inc(stackT_out.sem, 1)
                maxima(k, 2)
                maxima(k, 3)
                neg_in_parts(k)
                for u in range(3, NU):
                    if ffn2 and u % 2 == 1:
                        scale_out(k, (u - 3) // 2)
                    if u == 4:
                        negT_copy(k)
                    if u in (4, 6, 8, 10):
                        batch_sums(k, (u - 4) // 2)
                    if u % TT == 1 and u > TT:
                        take_Y(k, u // TT - 1)
                    if u == 12:
                        v_norms(k)
                take_Y(k, NHG - 1)
                if ffn2:
                    scale_out(k, NB - 1)
                finish_attention(k)
                for pr in range(4):
                    add_bias(k, pr)
                dve.wait_ge(proj_ready.sem, proj_ready.at(k, 1))
                dve.wait_ge(xa_in.sem, xa_in.at(k, 1))
                nc.vector.tensor_tensor(x_attn[:].rearrange("p t c -> p (t c)"), M0[:],
                                        x_attn[:].rearrange("p t c -> p (t c)"), ALU.add).then_inc(xa_sum.sem, 1)
                flash(k)

            def center(n):
                dve.wait_ge(x_in[n].sem, x_in[n].at(0, 1))
                nc.vector.tensor_reduce(ln_sum[:, n, :], x_stage[:, n], axis=AX.X, op=ALU.add).then_inc(p_sum.sem, 1)
                dve.wait_ge(p_sum.sem, p_sum.at(0, n + 1))
                nc.vector.tensor_scalar(ln_mean[:, n, :], ln_sum[:, n, :], 1.0 / C, None, ALU.mult).then_inc(p_mean.sem, 1)
                dve.wait_ge(p_mean.sem, p_mean.at(0, n + 1))
                nc.vector.tensor_tensor(x_stage[:, n], x_stage[:, n], ln_mean[:, n, :].unsqueeze(2).to_broadcast([P, TT, C]),
                                        ALU.subtract).then_inc(p_cent.sem, 1)

            def variance(n):
                dve.wait_ge(p_sq.sem, p_sq.at(0, n + 1))
                nc.vector.tensor_reduce(ln_var[:, n, :], ln_sq[:, n], axis=AX.X, op=ALU.add).then_inc(p_var.sem, 1)
                dve.wait_ge(p_var.sem, p_var.at(0, n + 1))
                nc.vector.tensor_scalar(ln_var[:, n, :], ln_var[:, n, :], 1.0 / C, LN_EPS, ALU.mult, ALU.add).then_inc(p_eps.sem, 1)

            def lower_half(n):
                dve.wait_ge(p_Th.sem, p_Th.at(0, n + 1))
                nc.vector.tensor_tensor(xnT_l[:, n * NT:(n + 1) * NT], L[n % 2][:],
                                        xnT_h[:, n * NT:(n + 1) * NT].bitcast(F32), ALU.subtract).then_inc(p_Tl.sem, 1)

            for n in range(NB + 3):
                if n < NB:
                    center(n)
                if 1 <= n <= NB:
                    variance(n - 1)
                if n == 2:
                    dve.wait_ge(p_wh.sem, p_wh.at(0, 1))
                    nc.vector.tensor_tensor(wq_l[:], M0[:, 0:3 * C], wq_h[:].bitcast(F32), ALU.subtract).then_inc(p_wl.sem, 1)
                if n >= 3:
                    lower_half(n - 3)
            dve.wait_ge(consts.sem, consts.at(0, 12))
            stage(0, False)
            with dve.Fori(1, NS) as k:
                stage(k, True)
            keep_phi(NS)
            dve.wait_ge(Zrun_out.sem, Zrun_out.at(NS - 1, 3))
            nc.vector.reciprocal(Z_run[:], Z_run[:]).then_inc(fin_rz.sem, 1)
            dve.wait_ge(fin_rz.sem, fin_rz.at(0, 1))
            for n in range(NB):
                scale_out(NS, n)
                dve.wait_ge(accB_out.sem, accB_out.at(NS, n + 1))
                nc.vector.tensor_tensor(acc[:, n], acc[:, n], Z_run[:, :, n:n + 1].to_broadcast([P, TT, C]),
                                        ALU.mult).then_inc(fin_mul.sem, 1)

        @block.gpsimd
        def _(gp):
            def identity(t, at):
                nc.gpsimd.memset(t[:], 0.0).then_inc(consts.sem, 1)
                gp.wait_ge(consts.sem, at)
                nc.gpsimd.affine_select(out=t[:], in_=t[:], compare_op=ALU.not_equal, fill=1.0, base=0,
                                        pattern=[[-1, P]], channel_multiplier=1).then_inc(consts.sem, 1)

            def scale_acc(k, n):
                nc.gpsimd.tensor_tensor(acc[:, n], acc[:, n], ab[:, 0, :, n:n + 1].to_broadcast([P, TT, C]),
                                        ALU.mult).then_inc(accA_out.sem, 1)

            def add_acc(k, n):
                gp.wait_ge(scaled_out.sem, scaled_out.at(k, n + 1))
                gp.wait_ge(accA_out.sem, accA_out.at(k, n + 1))
                nc.gpsimd.tensor_tensor(acc[:, n], acc[:, n], o_scaled[:], ALU.add).then_inc(accB_out.sem, 1)

            def subtract_max(k, t):
                gp.wait_ge(Z_out.sem, Z_out.at(k, NB * (t + 1)))
                gp.wait_ge(bmax_out.sem, bmax_out.at(k, t + 1))
                nc.gpsimd.tensor_tensor(D[:, t], D[:, t], batch_max[:, t % 2, :].unsqueeze(1).to_broadcast([P, NB, SW]),
                                        ALU.subtract).then_inc(sub_out.sem, 1)

            def dispatch(k, t):
                gp.wait_ge(brec_out.sem, brec_out.at(k, t + 1))
                nc.gpsimd.tensor_tensor(D[:, t], D[:, t], batch_sum[:, t % 2, :].unsqueeze(1).to_broadcast([P, NB, SW]),
                                        ALU.mult).then_inc(disp_out.sem, 1)

            def stage(k, ffn2):
                gp.wait_ge(ms_out.sem, ms_out.at(k, 2))
                nc.gpsimd.tensor_tensor(rms[:], mean_sq[:], minus_half[:], ALU.pow).then_inc(rms_out.sem, 1)
                gp.wait_ge(rms_out.sem, rms_out.at(k, 1))
                r = rms[:].rearrange("p (t a h) -> p t a h", t=TT, a=2)
                for which in range(2):
                    nc.gpsimd.tensor_tensor(
                        work[:, which].rearrange("p t (h d) -> p t h d", d=DH),
                        qkv[:, :, which * C:(which + 1) * C].rearrange("p t (h d) -> p t h d", d=DH),
                        r[:, :, which, :].unsqueeze(3).to_broadcast([P, TT, H, DH]), ALU.mult).then_inc(normed_out.sem, 1)
                subtract_max(k, 0)
                subtract_max(k, 1)
                gp.wait_ge(stack_out.sem, stack_out.at(k, 2))
                nc.gpsimd.tensor_tensor(work[:, 0].rearrange("p t (h d) -> p t h d", d=DH), V_v, V_v, ALU.mult).then_inc(vsq_out.sem, 1)
                subtract_max(k, 2)
                subtract_max(k, 3)
                if ffn2:
                    gp.wait_ge(ab_out.sem, ab_out.at(k - 1, 1))
                    for n in range(NB):
                        scale_acc(k, n)
                for t in range(TT):
                    if ffn2:
                        add_acc(k, t)
                    dispatch(k, t)
                if ffn2:
                    for n in range(TT, NB):
                        add_acc(k, n)
                gp.wait_ge(ab_out.sem, ab_out.at(k, 1))
                nc.gpsimd.tensor_tensor(Zs[:], Z[:], ab[:, 1], ALU.mult).then_inc(Zrun_out.sem, 1)
                nc.gpsimd.tensor_tensor(Z_run[:], Z_run[:], ab[:, 0], ALU.mult).then_inc(Zrun_out.sem, 1)
                gp.wait_ge(Zrun_out.sem, Zrun_out.at(k, 2))
                nc.gpsimd.tensor_tensor(Z_run[:], Z_run[:], Zs[:], ALU.add).then_inc(Zrun_out.sem, 1)

            nc.gpsimd.memset(minus_half[:], -0.5).then_inc(consts.sem, 1)
            nc.gpsimd.memset(Z_run[:], 0.0).then_inc(consts.sem, 1)
            identity(ident, 3)
            for m in range(NB + 1):
                if m < NB:
                    gp.wait_ge(p_cent.sem, p_cent.at(0, m + 1))
                    nc.gpsimd.tensor_tensor(ln_sq[:, m], x_stage[:, m], x_stage[:, m], ALU.mult).then_inc(p_sq.sem, 1)
                if m == 0:
                    continue
                n = m - 1
                gp.wait_ge(p_eps.sem, p_eps.at(0, n + 1))
                nc.gpsimd.tensor_tensor(ln_rstd[:, n, :], ln_var[:, n, :], minus_half[:, 0:TT], ALU.pow).then_inc(p_rstd.sem, 1)
                gp.wait_ge(p_rstd.sem, p_rstd.at(0, n + 1))
                nc.gpsimd.tensor_tensor(xn[:, n * TT:(n + 1) * TT, :], x_stage[:, n],
                                        ln_rstd[:, n, :].unsqueeze(2).to_broadcast([P, TT, C]), ALU.mult).then_inc(p_xn.sem, 1)
            identity(ident16, 5)
            identity(identb, 7)
            gp.wait_ge(p_var.sem, p_var.at(0, NB))
            nc.gpsimd.memset(m_run[:], -1e30).then_inc(consts.sem, 1)
            nc.gpsimd.memset(acc[:], 0.0).then_inc(consts.sem, 1)
            nc.gpsimd.memset(V1[:], 1.0).then_inc(consts.sem, 1)
            nc.gpsimd.memset(pick[:], 0.0).then_inc(picks.sem, 1)
            for q in range(3):
                gp.wait_ge(picks.sem, picks.at(0, q + 1))
                last = nc.gpsimd.affine_select(out=pick[:], in_=pick[:], compare_op=ALU.not_equal, fill=1.0, base=-NB * q,
                                               pattern=[[-1, NB], [0, P]], channel_multiplier=1)
                last.then_inc(picks.sem if q < 2 else consts.sem, 1)
            gp.wait_ge(consts.sem, 12)
            stage(0, False)
            with gp.Fori(1, NS) as k:
                stage(k, True)
            gp.wait_ge(ab_out.sem, ab_out.at(NS - 1, 1))
            for n in range(NB):
                scale_acc(NS, n)
            for n in range(NB):
                add_acc(NS, n)
                if n == 0:
                    gp.wait_ge(xa_back.sem, xa_back.at(0, 1))
                gp.wait_ge(fin_mul.sem, fin_mul.at(0, n + 1))
                nc.gpsimd.tensor_tensor(acc[:, n], acc[:, n], x_stage[:, n], ALU.add).then_inc(fin_add.sem, 1)


_INS = ["L0_attn_x", "L0_attn_w_qkv", "L0_attn_w_proj", "L0_ffn_phi", "L0_ffn_W", "L0_ffn_b"]


def kernel(**inputs):
    import numpy as _np
    import concourse.bacc as _bacc
    from concourse import mybir as _mybir
    from concourse.bass_utils import run_bass_kernel_spmd as _run

    nc = _bacc.Bacc("TRN2", target_bir_lowering=False, num_devices=1)
    arrays, args = {}, []
    for name in _INS:
        a = _np.ascontiguousarray(inputs[name])
        arrays[f"in_{name}"] = a
        args.append(nc.dram_tensor(f"in_{name}", a.shape, _mybir.dt.from_np(a.dtype), kind="ExternalInput").ap())
    result = nc.dram_tensor("result", (NB, NT, C), F32, kind="ExternalOutput").ap()
    program(nc, *args, result)
    r = _run(nc, [arrays], core_ids=[0])
    return r.results[0]["result"]
```

```python
from contextlib import ExitStack

import concourse.bass as bass
from concourse import mybir

F32 = mybir.dt.float32
F32R = mybir.dt.float32r
F16 = mybir.dt.float16
I32 = mybir.dt.int32
BF16 = mybir.dt.bfloat16
ALU = mybir.AluOpType
ACT = mybir.ActivationFunctionType
AX = mybir.AxisListType

P = 128
NB, NT, C = 8, 512, 128
H, DH = 16, 8
NE, NP = 64, 32
S = NE * NP
TT = NT // P
SW = 256
NS = S // SW
SUB = SW // P
EC = SW // NP
HG = 4
NHG = H // HG
PAD = 32
VC = DH + 1
VW = (H - 1) * VC + PAD + 1
NU = NHG * TT
RMS_EPS = 1.1920928955078125e-07
LN_EPS = 1e-5
NORM_EPS2 = 1e-24
SCALE = DH ** -0.5
RSQRT_GUESS = float(0x5F3759DF)
assert NU == NB * SUB and NS == NB and EC * NE // EC == NE


LOGITS = (3, 3, 3, 3, 2, 2)
FFN2_FROM = len(LOGITS)
assert sum(LOGITS) == NU and FFN2_FROM + NB <= NU


ROW_SUMS = (0, 0, 0, 3, 3, 3, 4, 4, 4, 4, 4, 3)
DISPATCH_EXP = {7: 0, 9: 1, 11: 2, 13: 3}
NEG_STEP = FFN2_FROM + 2
STACK_STEP = 10
assert sum(ROW_SUMS) == TT * NB


def half_of(counts, u, half):
    if u >= len(counts):
        return range(0)
    start, mid = sum(counts[:u]), sum(counts[:u]) + (counts[u] + 1) // 2
    return range(mid, start + counts[u]) if half else range(start, mid)


class Signal:

    def __init__(self, ctx, nc, name, per, first=0, by=1):
        self.sem = ctx.enter_context(nc.semaphore(name))
        self.per, self.first, self.by = per, first, by

    def at(self, k, n):
        return (k - self.first) * (self.per * self.by) + n * self.by


def later(k):
    return not isinstance(k, int) or k > 0


def program(nc, x, w_qkv, w_proj, phi, W, b, out):
    ctx = ExitStack()
    with ctx:
        def sb(name, shape, dt=F32):
            return ctx.enter_context(nc.sbuf_tensor(name, shape, dt))

        def sig(name, per, first=0, by=1):
            return Signal(ctx, nc, name, per, first, by)

        xn = sb("xn", [P, NB * TT, C])
        xnT_h = sb("xnT_h", [P, NB * NT], F32R)
        xnT_l = sb("xnT_l", [P, NB * NT], F32R)
        D = sb("D", [P, TT, NB, SW])
        acc = sb("acc", [P, NB, TT, C])
        phi_raw = sb("phi_raw", [P, SW])
        phi1_h, phi1_l = sb("phi1_h", [P, SW], F32R), sb("phi1_l", [P, SW], F32R)
        phi2_h, phi2_l = sb("phi2_h", [P, SW], F32R), sb("phi2_l", [P, SW], F32R)
        W_sb = sb("W_sb", [P, EC, C])
        bias_sb = sb("bias_sb", [P, SUB, C])
        slots_sb = sb("slots_sb", [P, 2, 2, SW])
        y = sb("y", [P, NB, SUB, C])
        E2 = sb("E2", [P, 4, NT])
        oT_sb = sb("oT_sb", [P, 2, NT])
        o_scaled = sb("o_scaled", [P, TT, C])
        over_batches = sb("over_batches", [P, TT, SW])
        row_max = sb("row_max", [P, TT, NB])
        neg_max = sb("neg_max", [P, TT, NB])
        neg_rest = sb("neg_rest", [P, 2, TT, NB])
        neg_parts = sb("neg_parts", [P, TT, 3, NB], BF16)
        negT = sb("negT", [TT * 3 * NB, P], BF16)
        neg_rows = sb("neg_rows", [3 * NB, NT], BF16)
        pick = sb("pick", [3 * NB, NB, P], BF16)
        dump = sb("dump", [P, 4, SW], BF16)
        Z = sb("Z", [P, TT, NB])
        Zs = sb("Zs", [P, TT, NB])
        Z_run = sb("Z_run", [P, TT, NB])
        m_run = sb("m_run", [P, TT, NB])
        m_new = sb("m_new", [P, TT, NB])
        ab_log = sb("ab_log", [P, 2, TT, NB])
        ab = sb("ab", [P, 2, TT, NB])
        ident = sb("ident", [P, P])
        ident16 = sb("ident16", [P, P], F16)
        identb = sb("identb", [P, P], BF16)
        minus_half = sb("minus_half", [P, P])
        wq_h, wq_l = sb("wq_h", [P, 3 * C], F32R), sb("wq_l", [P, 3 * C], F32R)
        wp = sb("wp", [P, C])
        xb_h, xb_l = sb("xb_h", [P, NT], F32R), sb("xb_l", [P, NT], F32R)
        qkv = sb("qkv", [P, TT, 3 * C])
        work = sb("work", [P, 2, TT, C])
        mean_sq = sb("mean_sq", [P, P])
        rms = sb("rms", [P, P])
        rms_step = sb("rms_step", [P, P])
        stack = sb("stack", [P, 2, TT * H, 4, DH], F16)
        stackT = sb("stackT", [P, 2, NHG, NT], F16)
        V1 = sb("V1", [P, TT, VW])
        probs = sb("probs", [P, 4, 2, NT])
        yT_sb = sb("yT_sb", [P, 2, NT])
        Y = sb("Y", [P, TT, H, VC])
        vv = sb("vv", [P, TT * H])
        dots = sb("dots", [P, TT * H])
        inv_den = sb("inv_den", [P, TT * H])
        AO = work[:, 0]
        AOT = yT_sb[:, 0]
        x_attn = sb("x_attn", [P, TT, C])
        ln_sum = sb("ln_sum", [P, NB, TT])
        ln_mean = sb("ln_mean", [P, NB, TT])
        ln_var = sb("ln_var", [P, NB, TT])
        ln_rstd = sb("ln_rstd", [P, NB, TT])

        def bank(name):
            return ctx.enter_context(nc.psum_tensor(name, [P, 512], F32))

        sc = ctx.enter_context(nc.psum_tensor("sc", [P, 2, 512], F32))
        pvb = bank("pvb")
        L = [bank("L0"), bank("L1")]
        Fb = bank("Fb")
        M0 = bank("M0")
        M1 = bank("M1")
        y_bank = [pvb, M1]

        x_in = [sig(f"x_in{n}", 1, by=16) for n in range(NB)]
        w_in = sig("w_in", 2, by=16)
        phi_in = sig("phi_in", 1, by=16)
        W_in = sig("W_in", 1, by=16)
        bias_in = sig("bias_in", SUB, by=16)
        xb_in = sig("xb_in", 2, by=16)
        xa_in = sig("xa_in", 1, by=16)
        neg_in = sig("neg_in", TT, by=16)
        xa_out = sig("xa_out", 1, by=16)
        xa_back = sig("xa_back", 1, by=16)
        stored = sig("stored", NB, by=16)
        consts, picks = sig("consts", 12), sig("picks", 3)
        p_sum, p_mean, p_cent = sig("p_sum", NB), sig("p_mean", NB), sig("p_cent", NB)
        p_sq, p_var, p_eps = sig("p_sq", NB), sig("p_var", NB), sig("p_eps", NB)
        p_rstd, p_xn = sig("p_rstd", NB), sig("p_xn", NB)
        p_T, p_Th, p_Tl = sig("p_T", NB), sig("p_Th", NB), sig("p_Tl", NB)
        p_wT, p_wh, p_wl = sig("p_wT", 2), sig("p_wh", 2), sig("p_wl", 1)
        qkv_ready, logits_ready, stackT_ready = sig("qkv_ready", TT), sig("logits_ready", NU), sig("stackT_ready", 4)
        scores_ready, pv_done, yT_ready = sig("scores_ready", 2 * NU), sig("pv_done", NU), sig("yT_ready", NHG)
        lgT_ready, o_done, oT_ready = sig("lgT_ready", NU, 1), sig("o_done", NU, 1), sig("oT_ready", NB, 1)
        negT_ready, slots_ready, y_ready = sig("negT_ready", 1), sig("slots_ready", 4), sig("y_ready", 4)
        aoT_ready, proj_ready = sig("aoT_ready", 1), sig("proj_ready", 1)
        qkv_out, D_out, V_out = sig("qkv_out", TT), sig("D_out", NU), sig("V_out", 1)
        probs_out, Z_out, E_out = sig("probs_out", 2 * NU), sig("Z_out", TT * NB), sig("E_out", 2 * TT)
        E2_out, oT_out, yT_out = sig("E2_out", NU, 1), sig("oT_out", NB, 1), sig("yT_out", NHG)
        slots_out, AOT_out, ab_out = sig("slots_out", 4), sig("AOT_out", 1), sig("ab_out", 1)
        phi2_out, phi1h_out, phi1_out = sig("phi2_out", 2, 1), sig("phi1h_out", 1), sig("phi1_out", 1)
        sq_out, ms_out, half_out, stack_out = sig("sq_out", 1), sig("ms_out", 2), sig("half_out", 2), sig("stack_out", 2)
        rmax_out, bmax_out, nmax_out = sig("rmax_out", TT), sig("bmax_out", TT), sig("nmax_out", TT)
        rms_out = sig("rms_out", 11)
        parts_out, negT_out = sig("parts_out", 5), sig("negT_out", 1)
        bsum_out, brec_out = sig("bsum_out", TT), sig("brec_out", TT)
        stackT_out, Y_out, scaled_out = sig("stackT_out", 4), sig("Y_out", NHG), sig("scaled_out", NB, 1)
        vv_out, post_out, AO_out = sig("vv_out", 3), sig("post_out", 6), sig("AO_out", 1)
        y_out, xa_sum, flash_out = sig("y_out", 4), sig("xa_sum", 1), sig("flash_out", 4)
        fin_rz, fin_mul = sig("fin_rz", 1), sig("fin_mul", NB)
        normed_out, vsq_out = sig("normed_out", 2), sig("vsq_out", 1)
        sub_out, disp_out = sig("sub_out", TT), sig("disp_out", TT)
        accA_out, accB_out, Zrun_out = sig("accA_out", NB, 1), sig("accB_out", NB, 1), sig("Zrun_out", 3)
        fin_add = sig("fin_add", NB)

        x_stage = D[:, 0:2].rearrange("p a b s -> p (a b s)").rearrange("p (b t c) -> p b t c", b=NB, t=TT)
        w_stage = probs[:, 0, 0, 0:3 * C].rearrange("p (r c) -> p r c", r=3)
        wp_stage = probs[:, 0, 1, 0:C]
        ln_sq = acc
        x_tiles = x.rearrange("b (t p) c -> p b t c", p=P)
        out_tiles = out.rearrange("b (t p) c -> p b t c", p=P)
        phi_v = phi.rearrange("d n s -> d (n s)")
        W_v = W.rearrange("n d e -> d n e")
        V_in = qkv[:, :, 2 * C:3 * C].rearrange("p t (h d) -> p t h d", h=H)
        V_v = V1[:, :, 0:H * VC].rearrange("p t (h d) -> p t h d", h=H)[:, :, :, 0:DH]

        def per_head(t):
            return t.rearrange("p (t h) -> p t h", t=TT).unsqueeze(3).to_broadcast([P, TT, H, DH])

        block = ctx.enter_context(nc.Block())

        @block.sync
        def _(sp):
            def load_phi(k):
                if later(k):
                    sp.wait_ge(phi1_out.sem, phi1_out.at(k - 1, 1))
                sp.dma_start(phi_raw[:], phi_v[:, bass.ds(k * SW, SW)]).then_inc(phi_in.sem, 16)

            def load_xb(k):
                if later(k):
                    sp.wait_ge(qkv_ready.sem, qkv_ready.at(k - 1, TT))
                for dst, src in ((xb_h, xnT_h), (xb_l, xnT_l)):
                    sp.dma_start(dst[:].bitcast(F32), src[:, bass.ds(k * NT, NT)].bitcast(F32)).then_inc(xb_in.sem, 16)

            def stage(k, phi_ahead, xb_ahead):
                if later(k):
                    sp.wait_ge(y_ready.sem, y_ready.at(k - 1, 4))
                sp.dma_start(W_sb[:], W_v[:, bass.ds(k * EC, EC), :]).then_inc(W_in.sem, 16)
                if later(k):
                    sp.wait_ge(y_out.sem, y_out.at(k - 1, 4))
                for u in range(SUB):
                    rows = b[bass.ds(k * EC + u * (P // NP), P // NP), :]
                    sp.dma_start(bias_sb[:, u, :], rows.unsqueeze(1).to_broadcast([P // NP, NP, C])).then_inc(bias_in.sem, 16)
                if later(k):
                    sp.wait_ge(xa_out.sem, xa_out.at(k - 1, 1))
                sp.dma_start(x_attn[:], tiles_of(x, k)).then_inc(xa_in.sem, 16)
                if phi_ahead:
                    load_phi(k + 1)
                if xb_ahead:
                    load_xb(k + 2)
                sp.wait_ge(negT_out.sem, negT_out.at(k, 1))
                if later(k):
                    sp.wait_ge(lgT_ready.sem, lgT_ready.at(k, NU))
                for t in range(TT):
                    rows = 3 * NB
                    sp.dma_start(neg_rows[:, t * P:(t + 1) * P], negT[t * rows:(t + 1) * rows, :]).then_inc(neg_in.sem, 16)
                sp.wait_ge(xa_sum.sem, xa_sum.at(k, 1))
                sp.dma_start(tiles_of(out, k), x_attn[:]).then_inc(xa_out.sem, 16)

            def tiles_of(t, k):
                return t[bass.ds(k, 1)].rearrange("b (t p) c -> p (b t) c", p=P)

            sp.dma_start(w_stage, w_qkv.rearrange("(r p) c -> p r c", p=P)).then_inc(w_in.sem, 16)
            sp.dma_start(wp_stage, w_proj).then_inc(w_in.sem, 16)
            for n in range(NB):
                sp.dma_start(x_stage[:, n], x_tiles[:, n]).then_inc(x_in[n].sem, 16)
            load_phi(0)
            sp.wait_ge(p_Th.sem, p_Th.at(0, 1))
            sp.wait_ge(p_Tl.sem, p_Tl.at(0, 1))
            load_xb(0)
            sp.wait_ge(p_Tl.sem, p_Tl.at(0, 3))
            load_xb(1)
            stage(0, True, True)
            with sp.Fori(1, NS - 2) as k:
                stage(k, True, True)
            stage(NS - 2, True, False)
            stage(NS - 1, False, False)
            sp.wait_ge(slots_ready.sem, slots_ready.at(NS - 1, 4))
            sp.wait_ge(xa_out.sem, xa_out.at(NS - 1, 1))
            sp.dma_start(x_stage, out_tiles).then_inc(xa_back.sem, 16)
            for n in range(NB):
                sp.wait_ge(fin_add.sem, fin_add.at(0, n + 1))
                sp.dma_start(out_tiles[:, n], acc[:, n]).then_inc(stored.sem, 16)
            sp.wait_ge(stored.sem, NB * 16)

        @block.tensor
        def _(pe):
            def halves(dst, parts, start=True, stop=True):
                for n, (st, mv) in enumerate(parts):
                    last = nc.tensor.matmul(dst, st, mv, start=start and n == 0, stop=stop and n == len(parts) - 1)
                return last

            def qkv_products(k, t):
                if t == 0:
                    pe.wait_ge(xb_in.sem, xb_in.at(k, 2))
                    if isinstance(k, int) and k == 1:
                        pe.wait_ge(qkv_out.sem, qkv_out.at(0, TT))
                else:
                    pe.wait_ge(qkv_out.sem, qkv_out.at(k, t))
                h, l = xb_h[:, t * P:(t + 1) * P], xb_l[:, t * P:(t + 1) * P]
                halves(M0[:, 0:3 * C], ((h, wq_h[:]), (h, wq_l[:]), (l, wq_h[:]))).then_inc(qkv_ready.sem, 1)

            def logits(k, i):
                t, pr = divmod(i, NB // 2)
                if i == 0:
                    pe.wait_ge(phi1_out.sem, phi1_out.at(k, 1))
                if i >= 2:
                    pe.wait_ge(D_out.sem, D_out.at(k, i - 1))
                for n in range(2):
                    at = (2 * pr + n) * NT + t * P
                    h, l = xnT_h[:, at:at + P], xnT_l[:, at:at + P]
                    last = halves(L[i % 2][:, n * SW:(n + 1) * SW],
                                  ((h, phi1_h[:]), (h, phi1_l[:]), (l, phi1_h[:])))
                last.then_inc(logits_ready.sem, 1)

            def stack_transposes(k, g):
                which, pair = divmod(g, 2)
                if g % 2 == 0:
                    pe.wait_ge(stack_out.sem, stack_out.at(k, which + 1))
                if g > 0:
                    pe.wait_ge(stackT_out.sem, stackT_out.at(k, g))
                for n in range(2):
                    for t in range(TT):
                        at = t * H + (2 * pair + n) * HG
                        last = nc.tensor.transpose(
                            Fb[:].bitcast(F16)[:, (n * TT + t) * P:(n * TT + t + 1) * P],
                            stack[:, which, at:at + HG].rearrange("p h f d -> p (h f d)"), ident16[:])
                last.then_inc(stackT_ready.sem, 1)

            def scores(k, pair):
                u, half = divmod(pair, 2)
                hg, kt = divmod(u, TT)
                if pair > 0:
                    pe.wait_ge(probs_out.sem, probs_out.at(k, pair))
                for n in range(2):
                    r = PAD * (2 * half + n)
                    last = nc.tensor.matmul(sc[:, n, :], stackT[r:r + PAD, 1, hg, kt * P:(kt + 1) * P],
                                            stackT[r:r + PAD, 0, hg, :], start=True, stop=True)
                last.then_inc(scores_ready.sem, 1)

            def pv(k, u):
                hg, kt = divmod(u, TT)
                pe.wait_ge(probs_out.sem, probs_out.at(k, 2 * u + 2))
                if u == 0:
                    pe.wait_ge(V_out.sem, V_out.at(k, 1))
                if u == 0 and later(k):
                    pe.wait_ge(y_out.sem, y_out.at(k - 1, 3))
                if kt == 0 and hg > 0:
                    pe.wait_ge(yT_out.sem, yT_out.at(k, hg))
                for j in range(HG):
                    at = (hg * HG + j) * VC
                    last = nc.tensor.matmul(pvb[PAD * j:PAD * (j + 1), :], V1[:, kt, at:at + PAD],
                                            probs[:, (2 * u + j // 2) % 4, j % 2, :],
                                            start=kt == 0, stop=kt == TT - 1)
                last.then_inc(pv_done.sem, 1)

            def yT_back(k, hg):
                pe.wait_ge(yT_out.sem, yT_out.at(k, hg + 1))
                if hg > 0:
                    pe.wait_ge(Y_out.sem, Y_out.at(k, hg))
                for t in range(TT):
                    last = nc.tensor.transpose(M0[:, t * P:(t + 1) * P], yT_sb[:, hg % 2, t * P:(t + 1) * P], ident[:])
                last.then_inc(yT_ready.sem, 1)

            def logits_T(k, v):
                n, u = divmod(v, SUB)
                if v == 0:
                    pe.wait_ge(phi2_out.sem, phi2_out.at(k, 2))
                    pe.wait_ge(neg_in.sem, neg_in.at(k - 1, TT))
                    pe.wait_ge(y_out.sem, y_out.at(k - 1, 4))
                else:
                    pe.wait_ge(E2_out.sem, E2_out.at(k, v))
                s, m = slice(u * P, (u + 1) * P), slice(n * NT, (n + 1) * NT)
                halves(Fb[:], ((phi2_h[:, s], xnT_h[:, m]), (phi2_h[:, s], xnT_l[:, m]),
                               (phi2_l[:, s], xnT_h[:, m]), (pick[:, n, :], neg_rows[:]))).then_inc(lgT_ready.sem, 1)

            def combine(k, v, attn):
                n, u = divmod(v, SUB)
                pe.wait_ge(E2_out.sem, E2_out.at(k, v + 1))
                if n < 2 and u == 0 and attn:
                    pe.wait_ge(D_out.sem, D_out.at(k, NU))
                if n >= 2 and u == 0:
                    pe.wait_ge(oT_out.sem, oT_out.at(k, n - 1))
                nc.tensor.matmul(L[n % 2][:], y[:, n, u, :], E2[:, v % 4, :],
                                 start=u == 0, stop=u == SUB - 1).then_inc(o_done.sem, 1)

            def oT_back(k, n):
                pe.wait_ge(oT_out.sem, oT_out.at(k, n + 1))
                if n >= 1:
                    pe.wait_ge(scaled_out.sem, scaled_out.at(k, n))
                elif k is NS:
                    pe.wait_ge(y_out.sem, y_out.at(k - 1, 4))
                else:
                    pe.wait_ge(negT_out.sem, negT_out.at(k, 1))
                for t in range(TT):
                    last = nc.tensor.transpose(M1[:, t * P:(t + 1) * P], oT_sb[:, n % 2, t * P:(t + 1) * P], ident[:])
                last.then_inc(oT_ready.sem, 1)

            def neg_transpose(k):
                if later(k):
                    pe.wait_ge(y_out.sem, y_out.at(k - 1, 4))
                pe.wait_ge(parts_out.sem, parts_out.at(k, 5))
                nc.tensor.transpose(M1[:].bitcast(BF16)[0:TT * 3 * NB, 0:P],
                                    neg_parts[:].rearrange("p t a b -> p (t a b)"), identb[:]).then_inc(negT_ready.sem, 1)

            def slots(k, pr, ffn2):
                if pr == 0:
                    pe.wait_ge(disp_out.sem, disp_out.at(k, TT))
                if pr < 2 and ffn2:
                    pe.wait_ge(oT_out.sem, oT_out.at(k, NB - 1 + pr))
                if pr < 2:
                    pe.wait_ge(D_out.sem, D_out.at(k, NU))
                else:
                    pe.wait_ge(slots_out.sem, slots_out.at(k, pr - 1))
                for n in range(2):
                    for t in range(TT):
                        last = nc.tensor.matmul(L[pr % 2][:, n * SW:(n + 1) * SW], xn[:, (2 * pr + n) * TT + t, :],
                                                D[:, t, 2 * pr + n, :], start=t == 0, stop=t == TT - 1)
                last.then_inc(slots_ready.sem, 1)

            def experts(k, pr, ffn2):
                pe.wait_ge(slots_out.sem, slots_out.at(k, pr + 1))
                if pr == 0:
                    pe.wait_ge(W_in.sem, W_in.at(k, 1))
                    pe.wait_ge(yT_out.sem, yT_out.at(k, NHG))
                if pr == 1 and ffn2:
                    pe.wait_ge(scaled_out.sem, scaled_out.at(k, NB))
                if pr == 1 and not ffn2:
                    pe.wait_ge(negT_out.sem, negT_out.at(k, 1))
                if pr >= 2:
                    pe.wait_ge(y_out.sem, y_out.at(k, pr - 1))
                for n in range(2):
                    for u in range(SUB):
                        for j in range(P // NP):
                            at = u * P + j * NP
                            last = nc.tensor.matmul(
                                y_bank[pr % 2][j * NP:(j + 1) * NP, (n * SUB + u) * C:(n * SUB + u + 1) * C],
                                slots_sb[:, pr % 2, n, at:at + NP], W_sb[:, u * (P // NP) + j, :], start=True, stop=True)
                last.then_inc(y_ready.sem, 1)

            def attention_transposes(k):
                pe.wait_ge(AO_out.sem, AO_out.at(k, 1))
                for t in range(TT):
                    last = nc.tensor.transpose(M0[:, t * P:(t + 1) * P], AO[:, t, :], ident[:])
                last.then_inc(aoT_ready.sem, 1)

            def project(k):
                pe.wait_ge(AOT_out.sem, AOT_out.at(k, 1))
                for t in range(TT):
                    last = nc.tensor.matmul(M0[:, t * C:(t + 1) * C], AOT[:, t * P:(t + 1) * P], wp[:], start=True, stop=True)
                last.then_inc(proj_ready.sem, 1)

            def ffn2_part(k, v):
                if v < NU:
                    logits_T(k, v)
                if v > 0:
                    combine(k, v - 1, k is not NS)

            def stage(k, ffn2, ahead):
                pe.wait_ge(stackT_out.sem, stackT_out.at(k, 4))
                for u in range(NU):
                    n = u - FFN2_FROM
                    for half in range(2):
                        scores(k, 2 * u + half)
                        for i in half_of(LOGITS, u, half):
                            logits(k, i)
                        if ffn2 and (0 <= n < NB or n == NB and half == 0):
                            ffn2_part(k, SUB * n + half)
                    if u > 0:
                        pv(k, u - 1)
                    if ahead and 1 <= u <= TT:
                        if u == 1 and later(k):
                            pe.wait_ge(xa_sum.sem, xa_sum.at(k - 1, 1))
                        qkv_products(k + 1, u - 1)
                    if u == NEG_STEP:
                        neg_transpose(k)
                    if ffn2 and n >= 2:
                        oT_back(k, n - 2)
                    if u % TT == 1 and u > TT:
                        if u == TT + 1 and ahead:
                            pe.wait_ge(qkv_out.sem, qkv_out.at(k + 1, TT))
                        yT_back(k, u // TT - 1)
                pv(k, NU - 1)
                slots(k, 0, ffn2)
                yT_back(k, NHG - 1)
                slots(k, 1, ffn2)
                experts(k, 0, ffn2)
                if ahead:
                    stack_transposes(k + 1, 0)
                slots(k, 2, ffn2)
                experts(k, 1, ffn2)
                if ahead:
                    stack_transposes(k + 1, 1)
                slots(k, 3, ffn2)
                if ahead:
                    stack_transposes(k + 1, 2)
                experts(k, 2, ffn2)
                attention_transposes(k)
                if ahead:
                    stack_transposes(k + 1, 3)
                experts(k, 3, ffn2)
                project(k)

            pe.wait_ge(consts.sem, consts.at(0, 4))
            pe.wait_ge(w_in.sem, w_in.at(0, 2))
            for r in range(3):
                last = nc.tensor.transpose(M0[:, r * P:(r + 1) * P], w_stage[:, r, :], ident[:])
            last.then_inc(p_wT.sem, 1)
            nc.tensor.transpose(M1[:, 0:P], wp_stage, ident[:]).then_inc(p_wT.sem, 1)
            for n in range(NB):
                pe.wait_ge(p_xn.sem, p_xn.at(0, n + 1))
                if n >= 2:
                    pe.wait_ge(p_Tl.sem, p_Tl.at(0, n - 1))
                for t in range(TT):
                    last = nc.tensor.transpose(L[n % 2][:, t * P:(t + 1) * P], xn[:, n * TT + t, :], ident[:])
                last.then_inc(p_T.sem, 1)
            pe.wait_ge(consts.sem, consts.at(0, 12))
            pe.wait_ge(p_wh.sem, p_wh.at(0, 2))
            pe.wait_ge(p_wl.sem, p_wl.at(0, 1))
            pe.wait_ge(p_Tl.sem, p_Tl.at(0, NB))
            for t in range(TT):
                qkv_products(0, t)
            for g in range(4):
                stack_transposes(0, g)
            stage(0, False, True)
            with pe.Fori(1, NS - 1) as k:
                stage(k, True, True)
            stage(NS - 1, True, False)
            for n in range(NB + 1):
                ffn2_part(NS, SUB * n)
                if n < NB:
                    ffn2_part(NS, SUB * n + 1)
                if n >= 1:
                    oT_back(NS, n - 1)

        @block.scalar
        def _(act):
            def copy(dst, src):
                return nc.scalar.activation(dst, src, ACT.Copy)

            def row_sum(k, at):
                t, n = divmod(at, NB)
                if n == 0:
                    act.wait_ge(nmax_out.sem, nmax_out.at(k, t + 1))
                if at == 0 and later(k):
                    act.wait_ge(Zrun_out.sem, Zrun_out.at(k - 1, 3))
                if at >= 4:
                    act.wait_ge(Z_out.sem, Z_out.at(k, at - 3))
                nc.scalar.activation(dump[:, at % 4, :], D[:, t, n, :], ACT.Exp, bias=neg_max[:, t, n:n + 1],
                                     accum_out=Z[:, t, n:n + 1]).then_inc(Z_out.sem, 1)

            def qkv_copy(k, t):
                act.wait_ge(qkv_ready.sem, qkv_ready.at(k, t + 1))
                copy(qkv[:, t, :], M0[:, 0:3 * C]).then_inc(qkv_out.sem, 1)

            def logits_copy(k, i):
                t, pr = divmod(i, NB // 2)
                act.wait_ge(logits_ready.sem, logits_ready.at(k, i + 1))
                copy(D[:, t, 2 * pr:2 * pr + 2, :].rearrange("p b s -> p (b s)"), L[i % 2][:]).then_inc(D_out.sem, 1)

            def dispatch_exp(k, t, half):
                if half == 0:
                    act.wait_ge(sub_out.sem, sub_out.at(k, t + 1))
                part = slice(half * NB // 2, (half + 1) * NB // 2)
                nc.scalar.activation(D[:, t, part], D[:, t, part], ACT.Exp).then_inc(E_out.sem, 1)

            def probabilities(k, pair):
                act.wait_ge(scores_ready.sem, scores_ready.at(k, pair + 1))
                if pair >= 4:
                    act.wait_ge(pv_done.sem, pv_done.at(k, pair // 2 - 1))
                nc.scalar.activation(probs[:, pair % 4], sc[:], ACT.Exp, scale=SCALE).then_inc(probs_out.sem, 1)

            def combine_exp(k, v):
                act.wait_ge(lgT_ready.sem, lgT_ready.at(k, v + 1))
                if v >= 4:
                    act.wait_ge(o_done.sem, o_done.at(k, v - 3))
                nc.scalar.activation(E2[:, v % 4, :], Fb[:], ACT.Exp).then_inc(E2_out.sem, 1)

            def oT_copy(k, n):
                act.wait_ge(o_done.sem, o_done.at(k, SUB * (n + 1)))
                if n >= 2:
                    act.wait_ge(oT_ready.sem, oT_ready.at(k, n - 1))
                copy(oT_sb[:, n % 2, :], L[n % 2][:]).then_inc(oT_out.sem, 1)

            def yT_copy(k, hg):
                act.wait_ge(pv_done.sem, pv_done.at(k, TT * (hg + 1)))
                if hg >= 2:
                    act.wait_ge(yT_ready.sem, yT_ready.at(k, hg - 1))
                copy(yT_sb[:, hg % 2, :], pvb[:]).then_inc(yT_out.sem, 1)

            def stage(k, ffn2, ahead):
                act.wait_ge(qkv_out.sem, qkv_out.at(k, TT))
                if later(k):
                    act.wait_ge(AO_out.sem, AO_out.at(k - 1, 1))
                copy(V_v, V_in).then_inc(V_out.sem, 1)
                for u in range(NU):
                    n = u - FFN2_FROM
                    for half in range(2):
                        probabilities(k, 2 * u + half)
                        for i in half_of(LOGITS, u, half):
                            logits_copy(k, i)
                        if ffn2 and 0 <= n < NB:
                            combine_exp(k, SUB * n + half)
                        for at in half_of(ROW_SUMS, u, half):
                            row_sum(k, at)
                        if u in DISPATCH_EXP:
                            dispatch_exp(k, DISPATCH_EXP[u], half)
                        if half == 0 and u % TT == 0 and u >= TT:
                            yT_copy(k, u // TT - 1)
                    if ahead and 1 <= u <= TT:
                        if u == 1:
                            act.wait_ge(V_out.sem, V_out.at(k, 1))
                            act.wait_ge(normed_out.sem, normed_out.at(k, 2))
                        qkv_copy(k + 1, u - 1)
                    if ffn2 and 1 <= n <= NB:
                        oT_copy(k, n - 1)
                yT_copy(k, NHG - 1)
                for pr in range(4):
                    act.wait_ge(slots_ready.sem, slots_ready.at(k, pr + 1))
                    if pr >= 2:
                        act.wait_ge(y_ready.sem, y_ready.at(k, pr - 1))
                    copy(slots_sb[:, pr % 2].rearrange("p n s -> p (n s)"), L[pr % 2][:]).then_inc(slots_out.sem, 1)
                act.wait_ge(aoT_ready.sem, aoT_ready.at(k, 1))
                copy(AOT, M0[:]).then_inc(AOT_out.sem, 1)
                act.wait_ge(flash_out.sem, flash_out.at(k, 4))
                if ffn2:
                    act.wait_ge(accB_out.sem, accB_out.at(k, NB))
                nc.scalar.activation(ab[:], ab_log[:], ACT.Exp).then_inc(ab_out.sem, 1)

            act.wait_ge(p_wT.sem, p_wT.at(0, 1))
            copy(wq_h[:], M0[:, 0:3 * C]).then_inc(p_wh.sem, 1)
            act.wait_ge(p_wT.sem, p_wT.at(0, 2))
            copy(wp[:], M1[:, 0:C]).then_inc(p_wh.sem, 1)
            for n in range(NB):
                act.wait_ge(p_T.sem, p_T.at(0, n + 1))
                copy(xnT_h[:, n * NT:(n + 1) * NT], L[n % 2][:]).then_inc(p_Th.sem, 1)
            act.wait_ge(consts.sem, consts.at(0, 12))
            act.wait_ge(p_xn.sem, p_xn.at(0, NB))
            for t in range(TT):
                qkv_copy(0, t)
            stage(0, False, True)
            with act.Fori(1, NS - 1) as k:
                stage(k, True, True)
            stage(NS - 1, True, False)
            for n in range(NB):
                combine_exp(NS, SUB * n)
                if n >= 1:
                    oT_copy(NS, n - 1)
                combine_exp(NS, SUB * n + 1)
            oT_copy(NS, NB - 1)

        @block.vector
        def _(dve):
            def keep_phi(k):
                if later(k - 1):
                    dve.wait_ge(lgT_ready.sem, lgT_ready.at(k - 1, NU))
                nc.vector.tensor_copy(phi2_h[:], phi1_h[:].bitcast(F32)).then_inc(phi2_out.sem, 1)
                nc.vector.tensor_copy(phi2_l[:], phi1_l[:].bitcast(F32)).then_inc(phi2_out.sem, 1)

            def split_phi(k):
                dve.wait_ge(phi_in.sem, phi_in.at(k, 1))
                nc.vector.tensor_copy(phi1_h[:], phi_raw[:]).then_inc(phi1h_out.sem, 1)
                dve.wait_ge(phi1h_out.sem, phi1h_out.at(k, 1))
                nc.vector.tensor_tensor(phi1_l[:], phi_raw[:], phi1_h[:].bitcast(F32), ALU.subtract).then_inc(phi1_out.sem, 1)

            def mean_squares(k):
                dve.wait_ge(qkv_out.sem, qkv_out.at(k, TT))
                qk = qkv[:, :, 0:2 * C]
                sq = work[:].rearrange("p a t c -> p (a t c)").rearrange("p (t c) -> p t c", t=TT)
                nc.vector.tensor_tensor(sq, qk, qk, ALU.mult).then_inc(sq_out.sem, 1)
                dve.wait_ge(sq_out.sem, sq_out.at(k, 1))
                nc.vector.tensor_reduce(mean_sq[:], work[:].rearrange("p a t c -> p (a t c)").rearrange(
                    "p (g d) -> p g d", d=DH), axis=AX.X, op=ALU.add).then_inc(ms_out.sem, 1)
                dve.wait_ge(ms_out.sem, ms_out.at(k, 1))
                nc.vector.tensor_scalar(mean_sq[:], mean_sq[:], 1.0 / DH, RMS_EPS, ALU.mult, ALU.add).then_inc(ms_out.sem, 1)

            def inverse_rms(k):
                dve.wait_ge(ms_out.sem, ms_out.at(k, 2))
                nc.vector.tensor_scalar(rms[:].bitcast(I32), mean_sq[:].bitcast(I32), -0.5, RSQRT_GUESS,
                                        ALU.mult, ALU.add).then_inc(rms_out.sem, 1)
                dve.wait_ge(rms_out.sem, rms_out.at(k, 1))
                nc.vector.tensor_scalar(mean_sq[:], mean_sq[:], -0.5, None, ALU.mult).then_inc(rms_out.sem, 1)
                for n in range(3):
                    dve.wait_ge(rms_out.sem, rms_out.at(k, 3 * n + 2))
                    nc.vector.tensor_tensor(rms_step[:], rms[:], rms[:], ALU.mult).then_inc(rms_out.sem, 1)
                    dve.wait_ge(rms_out.sem, rms_out.at(k, 3 * n + 3))
                    nc.vector.tensor_tensor(rms_step[:], rms_step[:], mean_sq[:], ALU.mult).then_inc(rms_out.sem, 1)
                    dve.wait_ge(rms_out.sem, rms_out.at(k, 3 * n + 4))
                    nc.vector.scalar_tensor_tensor(out=rms[:], in0=rms_step[:], scalar=1.5, in1=rms[:],
                                                   op0=ALU.add, op1=ALU.mult).then_inc(rms_out.sem, 1)

            def split_stack(k, which):
                dve.wait_ge(normed_out.sem, normed_out.at(k, which + 1))
                src = work[:, which].rearrange("p t (h d) -> p (t h) d", d=DH).unsqueeze(2).to_broadcast([P, TT * H, 2, DH])
                hi = stack[:, which, :, 0:2, :] if which == 0 else stack[:, which, :, 0:4:2, :]
                lo = stack[:, which, :, 2:4, :] if which == 0 else stack[:, which, :, 1:4:2, :]
                nc.vector.tensor_copy(hi, src).then_inc(half_out.sem, 1)
                dve.wait_ge(half_out.sem, half_out.at(k, which + 1))
                nc.vector.tensor_tensor(lo, src, hi, ALU.subtract).then_inc(stack_out.sem, 1)

            def maxima(k, t):
                dve.wait_ge(D_out.sem, D_out.at(k, 4 * (t + 1)))
                nc.vector.tensor_reduce(row_max[:, t, :], D[:, t], axis=AX.X, op=ALU.max).then_inc(rmax_out.sem, 1)
                nc.vector.tensor_reduce(over_batches[:, t, :], D[:, t].rearrange("p b s -> p s b"),
                                        axis=AX.X, op=ALU.max).then_inc(bmax_out.sem, 1)
                dve.wait_ge(rmax_out.sem, rmax_out.at(k, t + 1))
                nc.vector.tensor_scalar(neg_max[:, t, :], row_max[:, t, :], -1.0, None, ALU.mult).then_inc(nmax_out.sem, 1)

            def neg_in_parts(k):
                dve.wait_ge(nmax_out.sem, nmax_out.at(k, TT))
                nc.vector.tensor_copy(neg_parts[:, :, 0, :], neg_max[:]).then_inc(parts_out.sem, 1)
                dve.wait_ge(parts_out.sem, parts_out.at(k, 1))
                nc.vector.tensor_tensor(neg_rest[:, 0], neg_max[:], neg_parts[:, :, 0, :], ALU.subtract).then_inc(parts_out.sem, 1)
                dve.wait_ge(parts_out.sem, parts_out.at(k, 2))
                nc.vector.tensor_copy(neg_parts[:, :, 1, :], neg_rest[:, 0]).then_inc(parts_out.sem, 1)
                dve.wait_ge(parts_out.sem, parts_out.at(k, 3))
                nc.vector.tensor_tensor(neg_rest[:, 1], neg_rest[:, 0], neg_parts[:, :, 1, :], ALU.subtract).then_inc(parts_out.sem, 1)
                dve.wait_ge(parts_out.sem, parts_out.at(k, 4))
                nc.vector.tensor_copy(neg_parts[:, :, 2, :], neg_rest[:, 1]).then_inc(parts_out.sem, 1)

            def negT_copy(k):
                dve.wait_ge(negT_ready.sem, negT_ready.at(k, 1))
                if later(k):
                    dve.wait_ge(neg_in.sem, neg_in.at(k - 1, TT))
                nc.vector.tensor_copy(negT[:], M1[:].bitcast(BF16)[0:TT * 3 * NB, 0:P]).then_inc(negT_out.sem, 1)

            def batch_sums(k, t):
                dve.wait_ge(E_out.sem, E_out.at(k, 2 * t + 2))
                nc.vector.tensor_reduce(over_batches[:, t, :], D[:, t].rearrange("p b s -> p s b"),
                                        axis=AX.X, op=ALU.add).then_inc(bsum_out.sem, 1)
                dve.wait_ge(bsum_out.sem, bsum_out.at(k, t + 1))
                nc.vector.reciprocal(over_batches[:, t, :], over_batches[:, t, :]).then_inc(brec_out.sem, 1)

            def scale_out(k, n):
                dve.wait_ge(oT_ready.sem, oT_ready.at(k, n + 1))
                if n == 0:
                    dve.wait_ge(ab_out.sem, ab_out.at(k - 1, 1))
                else:
                    dve.wait_ge(accB_out.sem, accB_out.at(k, n))
                nc.vector.tensor_tensor(o_scaled[:], M1[:].rearrange("p (t c) -> p t c", t=TT),
                                        ab[:, 1, :, n:n + 1].to_broadcast([P, TT, C]), ALU.mult).then_inc(scaled_out.sem, 1)

            def take_Y(k, hg):
                dve.wait_ge(yT_ready.sem, yT_ready.at(k, hg + 1))
                nc.vector.tensor_copy(Y[:, :, hg * HG:(hg + 1) * HG, :],
                                      M0[:].rearrange("p (t j r) -> p t j r", t=TT, j=HG)[:, :, :, 0:VC]).then_inc(Y_out.sem, 1)

            def v_norms(k):
                dve.wait_ge(vsq_out.sem, vsq_out.at(k, 1))
                nc.vector.tensor_reduce(vv[:], work[:, 0].rearrange("p t (h d) -> p (t h) d", d=DH),
                                        axis=AX.X, op=ALU.add).then_inc(vv_out.sem, 1)
                dve.wait_ge(vv_out.sem, vv_out.at(k, 1))
                nc.vector.tensor_scalar(vv[:], vv[:], NORM_EPS2, None, ALU.max).then_inc(vv_out.sem, 1)
                dve.wait_ge(vv_out.sem, vv_out.at(k, 2))
                nc.vector.reciprocal(vv[:], vv[:]).then_inc(vv_out.sem, 1)

            def finish_attention(k):
                w0 = work[:, 0].rearrange("p t (h d) -> p t h d", d=DH)
                w1 = work[:, 1].rearrange("p t (h d) -> p t h d", d=DH)
                dve.wait_ge(Y_out.sem, Y_out.at(k, NHG))
                dve.wait_ge(vv_out.sem, vv_out.at(k, 3))
                nc.vector.tensor_tensor(w1, Y[:, :, :, 0:DH], V_v, ALU.mult).then_inc(post_out.sem, 1)
                nc.vector.reciprocal(inv_den[:].rearrange("p (t h) -> p t h", t=TT), Y[:, :, :, DH]).then_inc(post_out.sem, 1)
                dve.wait_ge(post_out.sem, post_out.at(k, 1))
                nc.vector.tensor_reduce(dots[:], work[:, 1].rearrange("p t (h d) -> p (t h) d", d=DH),
                                        axis=AX.X, op=ALU.add).then_inc(post_out.sem, 1)
                dve.wait_ge(post_out.sem, post_out.at(k, 3))
                nc.vector.tensor_tensor(dots[:], dots[:], vv[:], ALU.mult).then_inc(post_out.sem, 1)
                dve.wait_ge(post_out.sem, post_out.at(k, 4))
                nc.vector.tensor_tensor(w0, V_v, per_head(dots[:]), ALU.mult).then_inc(post_out.sem, 1)
                dve.wait_ge(post_out.sem, post_out.at(k, 5))
                nc.vector.tensor_tensor(w1, Y[:, :, :, 0:DH], w0, ALU.subtract).then_inc(post_out.sem, 1)
                dve.wait_ge(post_out.sem, post_out.at(k, 6))
                nc.vector.tensor_tensor(AO.rearrange("p t (h d) -> p t h d", d=DH), w1, per_head(inv_den[:]),
                                        ALU.mult).then_inc(AO_out.sem, 1)

            def add_bias(k, pr):
                dve.wait_ge(y_ready.sem, y_ready.at(k, pr + 1))
                if pr == 0:
                    dve.wait_ge(bias_in.sem, bias_in.at(k, SUB))
                nc.vector.tensor_tensor(
                    y[:, 2 * pr:2 * pr + 2].rearrange("p n u e -> p n (u e)"),
                    y_bank[pr % 2][:].rearrange("p (n f) -> p n f", n=2),
                    bias_sb[:].rearrange("p u e -> p (u e)").unsqueeze(1).to_broadcast([P, 2, SUB * C]),
                    ALU.add).then_inc(y_out.sem, 1)

            def flash(k):
                nc.vector.tensor_tensor(m_new[:], m_run[:], row_max[:], ALU.max).then_inc(flash_out.sem, 1)
                dve.wait_ge(flash_out.sem, flash_out.at(k, 1))
                nc.vector.tensor_tensor(ab_log[:, 0], m_run[:], m_new[:], ALU.subtract).then_inc(flash_out.sem, 1)
                nc.vector.tensor_tensor(ab_log[:, 1], row_max[:], m_new[:], ALU.subtract).then_inc(flash_out.sem, 1)
                dve.wait_ge(flash_out.sem, flash_out.at(k, 2))
                nc.vector.tensor_copy(m_run[:], m_new[:]).then_inc(flash_out.sem, 1)

            def stackT_copy(k, g):
                which, pair = divmod(g, 2)
                dve.wait_ge(stackT_ready.sem, stackT_ready.at(k, g + 1))
                nc.vector.tensor_copy(stackT[:, which, 2 * pair:2 * pair + 2, :].rearrange("p n m -> p (n m)"),
                                      Fb[:].bitcast(F16)).then_inc(stackT_out.sem, 1)

            def stage(k, ffn2, ahead):
                for u in range(1, NU):
                    n = u - FFN2_FROM
                    if u in (1, 2, 3, 5):
                        maxima(k, (1, 2, 3, 5).index(u))
                    if u == 5:
                        neg_in_parts(k)
                        take_Y(k, 0)
                        if ahead:
                            mean_squares(k + 1)
                            inverse_rms(k + 1)
                    if u - 1 in DISPATCH_EXP:
                        batch_sums(k, DISPATCH_EXP[u - 1])
                    if u == NEG_STEP:
                        negT_copy(k)
                    if ffn2 and n >= 2:
                        scale_out(k, n - 2)
                    if u == STACK_STEP and ahead:
                        split_stack(k + 1, 0)
                        split_stack(k + 1, 1)
                    if u in (9, 13):
                        take_Y(k, u // TT - 1)
                    if u == 14:
                        v_norms(k)
                        flash(k)
                        keep_phi(k + 1)
                        if ahead:
                            dve.wait_ge(phi2_out.sem, phi2_out.at(k + 1, 2))
                            dve.wait_ge(logits_ready.sem, logits_ready.at(k, NU))
                            split_phi(k + 1)
                take_Y(k, NHG - 1)
                finish_attention(k)
                add_bias(k, 0)
                if ahead:
                    stackT_copy(k + 1, 0)
                add_bias(k, 1)
                if ahead:
                    stackT_copy(k + 1, 1)
                    stackT_copy(k + 1, 2)
                add_bias(k, 2)
                if ahead:
                    stackT_copy(k + 1, 3)
                add_bias(k, 3)
                dve.wait_ge(proj_ready.sem, proj_ready.at(k, 1))
                dve.wait_ge(xa_in.sem, xa_in.at(k, 1))
                nc.vector.tensor_tensor(x_attn[:].rearrange("p t c -> p (t c)"), M0[:],
                                        x_attn[:].rearrange("p t c -> p (t c)"), ALU.add).then_inc(xa_sum.sem, 1)

            def center(n):
                dve.wait_ge(x_in[n].sem, x_in[n].at(0, 1))
                nc.vector.tensor_reduce(ln_sum[:, n, :], x_stage[:, n], axis=AX.X, op=ALU.add).then_inc(p_sum.sem, 1)
                dve.wait_ge(p_sum.sem, p_sum.at(0, n + 1))
                nc.vector.tensor_scalar(ln_mean[:, n, :], ln_sum[:, n, :], 1.0 / C, None, ALU.mult).then_inc(p_mean.sem, 1)
                dve.wait_ge(p_mean.sem, p_mean.at(0, n + 1))
                nc.vector.tensor_tensor(x_stage[:, n], x_stage[:, n], ln_mean[:, n, :].unsqueeze(2).to_broadcast([P, TT, C]),
                                        ALU.subtract).then_inc(p_cent.sem, 1)

            def variance(n):
                dve.wait_ge(p_sq.sem, p_sq.at(0, n + 1))
                nc.vector.tensor_reduce(ln_var[:, n, :], ln_sq[:, n], axis=AX.X, op=ALU.add).then_inc(p_var.sem, 1)
                dve.wait_ge(p_var.sem, p_var.at(0, n + 1))
                nc.vector.tensor_scalar(ln_var[:, n, :], ln_var[:, n, :], 1.0 / C, LN_EPS, ALU.mult, ALU.add).then_inc(p_eps.sem, 1)

            def lower_half(n):
                dve.wait_ge(p_Th.sem, p_Th.at(0, n + 1))
                nc.vector.tensor_tensor(xnT_l[:, n * NT:(n + 1) * NT], L[n % 2][:],
                                        xnT_h[:, n * NT:(n + 1) * NT].bitcast(F32), ALU.subtract).then_inc(p_Tl.sem, 1)

            for n in range(NB + 3):
                if n < NB:
                    center(n)
                if 1 <= n <= NB:
                    variance(n - 1)
                if n == 2:
                    dve.wait_ge(p_wh.sem, p_wh.at(0, 1))
                    nc.vector.tensor_tensor(wq_l[:], M0[:, 0:3 * C], wq_h[:].bitcast(F32), ALU.subtract).then_inc(p_wl.sem, 1)
                if n >= 3:
                    lower_half(n - 3)
            dve.wait_ge(consts.sem, consts.at(0, 12))
            split_phi(0)
            mean_squares(0)
            inverse_rms(0)
            split_stack(0, 0)
            split_stack(0, 1)
            for g in range(4):
                stackT_copy(0, g)
            stage(0, False, True)
            with dve.Fori(1, NS - 1) as k:
                stage(k, True, True)
            stage(NS - 1, True, False)
            dve.wait_ge(Zrun_out.sem, Zrun_out.at(NS - 1, 3))
            nc.vector.reciprocal(Z_run[:], Z_run[:]).then_inc(fin_rz.sem, 1)
            dve.wait_ge(fin_rz.sem, fin_rz.at(0, 1))
            for n in range(NB):
                scale_out(NS, n)
                dve.wait_ge(accB_out.sem, accB_out.at(NS, n + 1))
                nc.vector.tensor_tensor(acc[:, n], acc[:, n], Z_run[:, :, n:n + 1].to_broadcast([P, TT, C]),
                                        ALU.mult).then_inc(fin_mul.sem, 1)

        @block.gpsimd
        def _(gp):
            def identity(t, at):
                nc.gpsimd.memset(t[:], 0.0).then_inc(consts.sem, 1)
                gp.wait_ge(consts.sem, at)
                nc.gpsimd.affine_select(out=t[:], in_=t[:], compare_op=ALU.not_equal, fill=1.0, base=0,
                                        pattern=[[-1, P]], channel_multiplier=1).then_inc(consts.sem, 1)

            def scale_acc(k, n):
                nc.gpsimd.tensor_tensor(acc[:, n], acc[:, n], ab[:, 0, :, n:n + 1].to_broadcast([P, TT, C]),
                                        ALU.mult).then_inc(accA_out.sem, 1)

            def add_acc(k, n):
                gp.wait_ge(scaled_out.sem, scaled_out.at(k, n + 1))
                gp.wait_ge(accA_out.sem, accA_out.at(k, n + 1))
                nc.gpsimd.tensor_tensor(acc[:, n], acc[:, n], o_scaled[:], ALU.add).then_inc(accB_out.sem, 1)

            def subtract_max(k, t):
                gp.wait_ge(Z_out.sem, Z_out.at(k, NB * (t + 1)))
                gp.wait_ge(bmax_out.sem, bmax_out.at(k, t + 1))
                nc.gpsimd.tensor_tensor(D[:, t], D[:, t], over_batches[:, t, :].unsqueeze(1).to_broadcast([P, NB, SW]),
                                        ALU.subtract).then_inc(sub_out.sem, 1)

            def dispatch(k, t):
                gp.wait_ge(brec_out.sem, brec_out.at(k, t + 1))
                nc.gpsimd.tensor_tensor(D[:, t], D[:, t], over_batches[:, t, :].unsqueeze(1).to_broadcast([P, NB, SW]),
                                        ALU.mult).then_inc(disp_out.sem, 1)

            def normalise(k):
                gp.wait_ge(rms_out.sem, rms_out.at(k, 11))
                r = rms[:].rearrange("p (t a h) -> p t a h", t=TT, a=2)
                for which in range(2):
                    nc.gpsimd.tensor_tensor(
                        work[:, which].rearrange("p t (h d) -> p t h d", d=DH),
                        qkv[:, :, which * C:(which + 1) * C].rearrange("p t (h d) -> p t h d", d=DH),
                        r[:, :, which, :].unsqueeze(3).to_broadcast([P, TT, H, DH]), ALU.mult).then_inc(normed_out.sem, 1)

            def v_squares(k, ahead):
                if ahead:
                    gp.wait_ge(stack_out.sem, stack_out.at(k + 1, 2))
                gp.wait_ge(V_out.sem, V_out.at(k, 1))
                nc.gpsimd.tensor_tensor(work[:, 0].rearrange("p t (h d) -> p t h d", d=DH), V_v, V_v, ALU.mult).then_inc(vsq_out.sem, 1)

            def stage(k, ffn2, ahead):
                subtract_max(k, 0)
                if ffn2:
                    gp.wait_ge(ab_out.sem, ab_out.at(k - 1, 1))
                    for n in range(4):
                        scale_acc(k, n)
                if ahead:
                    normalise(k + 1)
                subtract_max(k, 1)
                if ffn2:
                    for n in range(4, NB):
                        scale_acc(k, n)
                dispatch(k, 0)
                if ffn2:
                    add_acc(k, 0)
                subtract_max(k, 2)
                if ffn2:
                    add_acc(k, 1)
                dispatch(k, 1)
                if ffn2:
                    add_acc(k, 2)
                    add_acc(k, 3)
                subtract_max(k, 3)
                v_squares(k, ahead)
                dispatch(k, 2)
                if ffn2:
                    add_acc(k, 4)
                    add_acc(k, 5)
                dispatch(k, 3)
                if ffn2:
                    add_acc(k, 6)
                    add_acc(k, 7)
                gp.wait_ge(ab_out.sem, ab_out.at(k, 1))
                nc.gpsimd.tensor_tensor(Zs[:], Z[:], ab[:, 1], ALU.mult).then_inc(Zrun_out.sem, 1)
                nc.gpsimd.tensor_tensor(Z_run[:], Z_run[:], ab[:, 0], ALU.mult).then_inc(Zrun_out.sem, 1)
                gp.wait_ge(Zrun_out.sem, Zrun_out.at(k, 2))
                nc.gpsimd.tensor_tensor(Z_run[:], Z_run[:], Zs[:], ALU.add).then_inc(Zrun_out.sem, 1)

            nc.gpsimd.memset(minus_half[:], -0.5).then_inc(consts.sem, 1)
            nc.gpsimd.memset(Z_run[:], 0.0).then_inc(consts.sem, 1)
            identity(ident, 3)
            for m in range(NB + 1):
                if m < NB:
                    gp.wait_ge(p_cent.sem, p_cent.at(0, m + 1))
                    nc.gpsimd.tensor_tensor(ln_sq[:, m], x_stage[:, m], x_stage[:, m], ALU.mult).then_inc(p_sq.sem, 1)
                if m == 0:
                    continue
                n = m - 1
                gp.wait_ge(p_eps.sem, p_eps.at(0, n + 1))
                nc.gpsimd.tensor_tensor(ln_rstd[:, n, :], ln_var[:, n, :], minus_half[:, 0:TT], ALU.pow).then_inc(p_rstd.sem, 1)
                gp.wait_ge(p_rstd.sem, p_rstd.at(0, n + 1))
                nc.gpsimd.tensor_tensor(xn[:, n * TT:(n + 1) * TT, :], x_stage[:, n],
                                        ln_rstd[:, n, :].unsqueeze(2).to_broadcast([P, TT, C]), ALU.mult).then_inc(p_xn.sem, 1)
            identity(ident16, 5)
            identity(identb, 7)
            gp.wait_ge(p_var.sem, p_var.at(0, NB))
            nc.gpsimd.memset(m_run[:], -1e30).then_inc(consts.sem, 1)
            nc.gpsimd.memset(acc[:], 0.0).then_inc(consts.sem, 1)
            nc.gpsimd.memset(V1[:], 1.0).then_inc(consts.sem, 1)
            nc.gpsimd.memset(pick[:], 0.0).then_inc(picks.sem, 1)
            for q in range(3):
                gp.wait_ge(picks.sem, picks.at(0, q + 1))
                last = nc.gpsimd.affine_select(out=pick[:], in_=pick[:], compare_op=ALU.not_equal, fill=1.0, base=-NB * q,
                                               pattern=[[-1, NB], [0, P]], channel_multiplier=1)
                last.then_inc(picks.sem if q < 2 else consts.sem, 1)
            gp.wait_ge(consts.sem, 12)
            normalise(0)
            stage(0, False, True)
            with gp.Fori(1, NS - 1) as k:
                stage(k, True, True)
            stage(NS - 1, True, False)
            gp.wait_ge(ab_out.sem, ab_out.at(NS - 1, 1))
            for n in range(NB):
                scale_acc(NS, n)
            for n in range(NB):
                add_acc(NS, n)
                if n == 0:
                    gp.wait_ge(xa_back.sem, xa_back.at(0, 1))
                gp.wait_ge(fin_mul.sem, fin_mul.at(0, n + 1))
                nc.gpsimd.tensor_tensor(acc[:, n], acc[:, n], x_stage[:, n], ALU.add).then_inc(fin_add.sem, 1)


_INS = ["L0_attn_x", "L0_attn_w_qkv", "L0_attn_w_proj", "L0_ffn_phi", "L0_ffn_W", "L0_ffn_b"]


def kernel(**inputs):
    import numpy as _np
    import concourse.bacc as _bacc
    from concourse import mybir as _mybir
    from concourse.bass_utils import run_bass_kernel_spmd as _run

    nc = _bacc.Bacc("TRN2", target_bir_lowering=False, num_devices=1)
    arrays, args = {}, []
    for name in _INS:
        a = _np.ascontiguousarray(inputs[name])
        arrays[f"in_{name}"] = a
        args.append(nc.dram_tensor(f"in_{name}", a.shape, _mybir.dt.from_np(a.dtype), kind="ExternalInput").ap())
    result = nc.dram_tensor("result", (NB, NT, C), F32, kind="ExternalOutput").ap()
    program(nc, *args, result)
    r = _run(nc, [arrays], core_ids=[0])
    return r.results[0]["result"]
```

```python
from contextlib import ExitStack

import concourse.bass as bass
from concourse import mybir

F32 = mybir.dt.float32
F32R = mybir.dt.float32r
F16 = mybir.dt.float16
I32 = mybir.dt.int32
BF16 = mybir.dt.bfloat16
ALU = mybir.AluOpType
ACT = mybir.ActivationFunctionType
AX = mybir.AxisListType

P = 128
NB, NT, C = 8, 512, 128
H, DH = 16, 8
NE, NP = 64, 32
S = NE * NP
TT = NT // P
SW = 256
NS = S // SW
SUB = SW // P
EC = SW // NP
HG = 4
NHG = H // HG
PAD = 32
CZ = C + 1
VC = DH + 1
VW = (H - 1) * VC + PAD + 1
NU = NHG * TT
RMS_EPS = 1.1920928955078125e-07
LN_EPS = 1e-5
NORM_EPS2 = 1e-24
SCALE = DH ** -0.5
RSQRT_GUESS = float(0x5F3759DF)
CONSTS = 13
assert NU == NB * SUB and NS == NB

LOGITS = (3, 3, 3, 3, 2, 2)
FFN2_FROM = len(LOGITS)
assert sum(LOGITS) == NU and FFN2_FROM + NB <= NU
DISPATCH_EXP = {6: 0, 7: 1, 9: 2, 10: 3}
NEG_STEP = FFN2_FROM + 2
BATCH_SUMS = {8: 0, 9: 1, 11: 2, 12: 3}
STACK_STEP = 10
ON_VECTOR = (2, 15)
ROW_MAXIMA = {1: (0, 1), 2: (2,), 3: (3, 4), 4: (5,), 5: (6,), 6: (7,)}
BATCH_MAXIMA = {2: 0, 3: 1, 4: 2, 6: 3}


def wide_pairs(k):
    return 2 * len(LOGITS) if later(k) else 2 * NU


def copier(i):
    return int(i in ON_VECTOR)


def copies(engine, i):
    return sum(copier(j) == engine for j in range(i + 1))


def half_of(counts, u, half):
    if u >= len(counts):
        return range(0)
    start, mid = sum(counts[:u]), sum(counts[:u]) + (counts[u] + 1) // 2
    return range(mid, start + counts[u]) if half else range(start, mid)


class Signal:

    def __init__(self, ctx, nc, name, per, first=0, by=1):
        self.sem = ctx.enter_context(nc.semaphore(name))
        self.per, self.first, self.by = per, first, by

    def at(self, k, n):
        return (k - self.first) * (self.per * self.by) + n * self.by


def later(k):
    return not isinstance(k, int) or k > 0


def program(nc, x, w_qkv, w_proj, phi, W, b, out):
    ctx = ExitStack()
    with ctx:
        def sb(name, shape, dt=F32):
            return ctx.enter_context(nc.sbuf_tensor(name, shape, dt))

        def sig(name, per, first=0, by=1):
            return Signal(ctx, nc, name, per, first, by)

        xn = sb("xn", [P, NB * TT, C])
        xnT_h = sb("xnT_h", [P, NB * NT], F32R)
        xnT_l = sb("xnT_l", [P, NB * NT], F32R)
        D = sb("D", [P, TT, NB, SW])
        acc = sb("acc", [P, NB, TT, CZ])
        phi_raw = sb("phi_raw", [P, SW])
        phi1_h, phi1_l = sb("phi1_h", [P, SW], F32R), sb("phi1_l", [P, SW], F32R)
        phi2_h, phi2_l = sb("phi2_h", [P, SW], F32R), sb("phi2_l", [P, SW], F32R)
        W_sb = sb("W_sb", [P, EC, C])
        bias_sb = sb("bias_sb", [P, SUB, C])
        slots_sb = sb("slots_sb", [P, 2, 2, SW])
        y = sb("y", [P, NB, SUB, CZ])
        E2 = sb("E2", [P, 4, NT])
        over_batches = sb("over_batches", [P, TT, SW])
        row_max = sb("row_max", [P, TT, NB])
        neg_max = sb("neg_max", [P, TT, NB])
        neg_rest = sb("neg_rest", [P, 2, TT, NB])
        neg_parts = sb("neg_parts", [P, TT, 3, NB], BF16)
        negT = sb("negT", [TT * 3 * NB, P], BF16)
        neg_rows = sb("neg_rows", [3 * NB, NT], BF16)
        pick = sb("pick", [3 * NB, NB, P], BF16)
        dump = sb("dump", [P, 4, C], BF16)
        inv_Z = sb("inv_Z", [P, NB, TT])
        m_run = sb("m_run", [P, TT, NB])
        m_new = sb("m_new", [P, TT, NB])
        ab_log = sb("ab_log", [P, 2, TT, NB])
        ab = sb("ab", [P, 2, TT, NB])
        ident = sb("ident", [P, P])
        ident16 = sb("ident16", [P, P], F16)
        identb = sb("identb", [P, P], BF16)
        minus_half = sb("minus_half", [P, TT])
        wq_h, wq_l = sb("wq_h", [P, 3 * C], F32R), sb("wq_l", [P, 3 * C], F32R)
        wp = sb("wp", [P, C])
        xb_h, xb_l = sb("xb_h", [P, NT], F32R), sb("xb_l", [P, NT], F32R)
        qkv = sb("qkv", [P, TT, 3 * C])
        work = sb("work", [P, 2, TT, C])
        mean_sq = sb("mean_sq", [P, P])
        rms = sb("rms", [P, P])
        rms_step = sb("rms_step", [P, P])
        stack = sb("stack", [P, 2, TT * H, 4, DH], F16)
        stackT = sb("stackT", [P, 2, NHG, NT], F16)
        V1 = sb("V1", [P, TT, VW])
        probs = sb("probs", [P, 4, 2, NT])
        yT_sb = sb("yT_sb", [P, 2, NT])
        Y = sb("Y", [P, TT, H, VC])
        vv = sb("vv", [P, TT * H])
        dots = sb("dots", [P, TT * H])
        inv_den = sb("inv_den", [P, TT * H])
        AO = work[:, 0]
        AOT = yT_sb[:, 0]
        x_attn = sb("x_attn", [P, TT, C])
        ln_sum = sb("ln_sum", [P, NB, TT])
        ln_neg_mean = sb("ln_neg_mean", [P, NB, TT])
        ln_var = sb("ln_var", [P, NB, TT])
        ln_rstd = sb("ln_rstd", [P, NB, TT])

        def bank(name):
            return ctx.enter_context(nc.psum_tensor(name, [P, 512], F32))

        sc = ctx.enter_context(nc.psum_tensor("sc", [P, 2, 512], F32))
        pvb = bank("pvb")
        L = [bank("L0"), bank("L1")]
        M0 = bank("M0")
        alt = ctx.enter_context(nc.psum_tensor("alt", [P, 2, 512], F32))
        Fb = alt[:, 0, :]
        M1 = alt[:, 1, :]
        y_bank = [pvb, M1]
        o_bank = [M1, L[0][:], L[1][:]]

        x_in = [sig(f"x_in{n}", 1, by=16) for n in range(NB)]
        w_in = sig("w_in", 2, by=16)
        phi_in = sig("phi_in", 1, by=16)
        W_in = sig("W_in", 1, by=16)
        bias_in = sig("bias_in", SUB, by=16)
        xb_in = sig("xb_in", 2, 1, by=16)
        xa_in = sig("xa_in", 1, by=16)
        neg_in = sig("neg_in", TT, by=16)
        xa_out = sig("xa_out", 1, by=16)
        xa_back = sig("xa_back", 1, by=16)
        stored = sig("stored", NB, by=16)
        consts, picks = sig("consts", CONSTS), sig("picks", 3)
        p_sum, p_mean, p_sq = sig("p_sum", NB), sig("p_mean", NB), sig("p_sq", NB * TT)
        p_eps, p_rstd, p_xn = sig("p_eps", NB), sig("p_rstd", NB), sig("p_xn", NB * TT)
        p_T, p_Th, p_Tl = sig("p_T", NB), sig("p_Th", NB), sig("p_Tl", NB)
        p_wT, p_wh, p_wl = sig("p_wT", 2), sig("p_wh", 2), sig("p_wl", 1)
        qkv_ready, logits_ready, stackT_ready = sig("qkv_ready", TT), sig("logits_ready", NU), sig("stackT_ready", 4)
        scores_ready, pv_done, yT_ready = sig("scores_ready", 2 * NU), sig("pv_done", NU), sig("yT_ready", NHG)
        lgT_ready, o_done = sig("lgT_ready", NU, 1), sig("o_done", 2 * NB, 1)
        negT_ready, slots_ready, y_ready = sig("negT_ready", 1), sig("slots_ready", 4), sig("y_ready", 4)
        aoT_ready, proj_ready = sig("aoT_ready", 1), sig("proj_ready", 1)
        qkv_out, V_out = sig("qkv_out", TT), sig("V_out", 1)
        D_out = [sig("D_out_scalar", copies(0, NU - 1)), sig("D_out_vector", copies(1, NU - 1))]
        probs_out, E_out = sig("probs_out", 2 * NU), sig("E_out", 2 * TT)
        E2_out, yT_out = sig("E2_out", NU, 1), sig("yT_out", NHG)
        slots_out, AOT_out, ab_out = sig("slots_out", 4), sig("AOT_out", 1), sig("ab_out", 1)
        phi2_out, phi1h_out, phi1_out = sig("phi2_out", 2, 1), sig("phi1h_out", 1), sig("phi1_out", 1)
        sq_out, ms_out, half_out, stack_out = sig("sq_out", 1), sig("ms_out", 2), sig("half_out", 2), sig("stack_out", 2)
        rmax_out, bmax_out, nmax_out = sig("rmax_out", 2 * TT), sig("bmax_out", TT), sig("nmax_out", 1)
        rms_out = sig("rms_out", 11)
        parts_out, negT_out = sig("parts_out", 5), sig("negT_out", 1)
        bsum_out, brec_out = sig("bsum_out", TT), sig("brec_out", TT)
        stackT_out, Y_out, accB_out = sig("stackT_out", 4), sig("Y_out", NHG), sig("accB_out", 2 * NB, 1)
        vv_out, post_out, AO_out = sig("vv_out", 3), sig("post_out", 6), sig("AO_out", 1)
        y_out, xa_sum, flash_out = sig("y_out", 4), sig("xa_sum", 1), sig("flash_out", 4)
        inv_Z_out, total_out = sig("inv_Z_out", 1), sig("total_out", NB)
        normed_out, vsq_out = sig("normed_out", 2), sig("vsq_out", 1)
        sub_out, disp_out = sig("sub_out", TT), sig("disp_out", TT)
        accA_out = sig("accA_out", NB, 1)

        x_stage = D[:, 0:2].rearrange("p a b s -> p (a b s)").rearrange("p (b t c) -> p b t c", b=NB, t=TT)
        w_stage = probs[:, 0, 0, 0:3 * C].rearrange("p (r c) -> p r c", r=3)
        wp_stage = probs[:, 0, 1, 0:C]
        x_tiles = x.rearrange("b (t p) c -> p b t c", p=P)
        out_tiles = out.rearrange("b (t p) c -> p b t c", p=P)
        phi_v = phi.rearrange("d n s -> d (n s)")
        W_v = W.rearrange("n d e -> d n e")
        V_in = qkv[:, :, 2 * C:3 * C].rearrange("p t (h d) -> p t h d", h=H)
        V_v = V1[:, :, 0:H * VC].rearrange("p t (h d) -> p t h d", h=H)[:, :, :, 0:DH]

        def stack_bank(k, g):
            return Fb if later(k) or g % 2 == 0 else pvb[:]

        def per_head(t):
            return t.rearrange("p (t h) -> p t h", t=TT).unsqueeze(3).to_broadcast([P, TT, H, DH])

        block = ctx.enter_context(nc.Block())

        @block.sync
        def _(sp):
            def load_phi(k):
                if later(k):
                    sp.wait_ge(phi1_out.sem, phi1_out.at(k - 1, 1))
                sp.dma_start(phi_raw[:], phi_v[:, bass.ds(k * SW, SW)]).then_inc(phi_in.sem, 16)

            def load_xb(k):
                if later(k - 1):
                    sp.wait_ge(qkv_ready.sem, qkv_ready.at(k - 1, TT))
                for dst, src in ((xb_h, xnT_h), (xb_l, xnT_l)):
                    sp.dma_start(dst[:].bitcast(F32), src[:, bass.ds(k * NT, NT)].bitcast(F32)).then_inc(xb_in.sem, 16)

            def stage(k, phi_ahead, xb_ahead):
                if later(k):
                    sp.wait_ge(y_ready.sem, y_ready.at(k - 1, 4))
                sp.dma_start(W_sb[:], W_v[:, bass.ds(k * EC, EC), :]).then_inc(W_in.sem, 16)
                if later(k):
                    sp.wait_ge(y_out.sem, y_out.at(k - 1, 4))
                for u in range(SUB):
                    rows = b[bass.ds(k * EC + u * (P // NP), P // NP), :]
                    sp.dma_start(bias_sb[:, u, :], rows.unsqueeze(1).to_broadcast([P // NP, NP, C])).then_inc(bias_in.sem, 16)
                if later(k):
                    sp.wait_ge(xa_out.sem, xa_out.at(k - 1, 1))
                sp.dma_start(x_attn[:], tiles_of(x, k)).then_inc(xa_in.sem, 16)
                if phi_ahead:
                    load_phi(k + 1)
                if xb_ahead:
                    load_xb(k + 2)
                sp.wait_ge(negT_out.sem, negT_out.at(k, 1))
                if later(k):
                    sp.wait_ge(lgT_ready.sem, lgT_ready.at(k, NU))
                for t in range(TT):
                    rows = 3 * NB
                    sp.dma_start(neg_rows[:, t * P:(t + 1) * P], negT[t * rows:(t + 1) * rows, :]).then_inc(neg_in.sem, 16)
                sp.wait_ge(xa_sum.sem, xa_sum.at(k, 1))
                sp.dma_start(tiles_of(out, k), x_attn[:]).then_inc(xa_out.sem, 16)

            def tiles_of(t, k):
                return t[bass.ds(k, 1)].rearrange("b (t p) c -> p (b t) c", p=P)

            sp.dma_start(w_stage, w_qkv.rearrange("(r p) c -> p r c", p=P)).then_inc(w_in.sem, 16)
            sp.dma_start(wp_stage, w_proj).then_inc(w_in.sem, 16)
            for n in range(NB):
                sp.dma_start(x_stage[:, n], x_tiles[:, n]).then_inc(x_in[n].sem, 16)
            load_phi(0)
            sp.wait_ge(p_Tl.sem, p_Tl.at(0, 3))
            load_xb(1)
            stage(0, True, True)
            with sp.Fori(1, NS - 2) as k:
                stage(k, True, True)
            stage(NS - 2, True, False)
            stage(NS - 1, False, False)
            sp.wait_ge(slots_ready.sem, slots_ready.at(NS - 1, 4))
            sp.wait_ge(xa_out.sem, xa_out.at(NS - 1, 1))
            sp.dma_start(x_stage, out_tiles).then_inc(xa_back.sem, 16)
            for n in range(NB):
                sp.wait_ge(total_out.sem, total_out.at(0, n + 1))
                sp.dma_start(out_tiles[:, n], acc[:, n, :, 0:C]).then_inc(stored.sem, 16)
            sp.wait_ge(stored.sem, NB * 16)

        @block.tensor
        def _(pe):
            def halves(dst, parts, start=True, stop=True):
                for n, (st, mv) in enumerate(parts):
                    last = nc.tensor.matmul(dst, st, mv, start=start and n == 0, stop=stop and n == len(parts) - 1)
                return last

            def qkv_products(k, t):
                if t == 0 and later(k):
                    pe.wait_ge(xb_in.sem, xb_in.at(k, 2))
                if t > 0:
                    pe.wait_ge(qkv_out.sem, qkv_out.at(k, t))
                src = (xb_h, xb_l) if later(k) else (xnT_h, xnT_l)
                h, l = src[0][:, t * P:(t + 1) * P], src[1][:, t * P:(t + 1) * P]
                halves(M0[:, 0:3 * C], ((h, wq_h[:]), (h, wq_l[:]), (l, wq_h[:]))).then_inc(qkv_ready.sem, 1)

            def logits(k, i):
                t, pr = divmod(i, NB // 2)
                if i == 0:
                    pe.wait_ge(phi1_out.sem, phi1_out.at(k, 1))
                if i >= 2:
                    out_by = D_out[copier(i - 2)]
                    pe.wait_ge(out_by.sem, out_by.at(k, copies(copier(i - 2), i - 2)))
                for n in range(2):
                    at = (2 * pr + n) * NT + t * P
                    h, l = xnT_h[:, at:at + P], xnT_l[:, at:at + P]
                    last = halves(L[i % 2][:, n * SW:(n + 1) * SW],
                                  ((h, phi1_h[:]), (h, phi1_l[:]), (l, phi1_h[:])))
                last.then_inc(logits_ready.sem, 1)

            def stack_transposes(k, g):
                which, pair = divmod(g, 2)
                if g % 2 == 0:
                    pe.wait_ge(stack_out.sem, stack_out.at(k, which + 1))
                if g > 0 and later(k) or g > 1:
                    pe.wait_ge(stackT_out.sem, stackT_out.at(k, g if later(k) else g - 1))
                for n in range(2):
                    for t in range(TT):
                        at = t * H + (2 * pair + n) * HG
                        last = nc.tensor.transpose(
                            stack_bank(k, g).bitcast(F16)[:, (n * TT + t) * P:(n * TT + t + 1) * P],
                            stack[:, which, at:at + HG].rearrange("p h f d -> p (h f d)"), ident16[:])
                last.then_inc(stackT_ready.sem, 1)

            def scores(k, pair):
                u, half = divmod(pair, 2)
                hg, kt = divmod(u, TT)
                bank = alt if pair < wide_pairs(k) and pair % 2 else sc
                if pair >= 2:
                    since = 2 if pair < wide_pairs(k) else 1
                    pe.wait_ge(probs_out.sem, probs_out.at(k, pair + 1 - since))
                if pair == 1 and later(k):
                    pe.wait_ge(y_out.sem, y_out.at(k - 1, 4))
                for n in range(2):
                    r = PAD * (2 * half + n)
                    last = nc.tensor.matmul(bank[:, n, :], stackT[r:r + PAD, 1, hg, kt * P:(kt + 1) * P],
                                            stackT[r:r + PAD, 0, hg, :], start=True, stop=True)
                last.then_inc(scores_ready.sem, 1)

            def pv(k, u):
                hg, kt = divmod(u, TT)
                pe.wait_ge(probs_out.sem, probs_out.at(k, 2 * u + 2))
                if u == 0:
                    pe.wait_ge(V_out.sem, V_out.at(k, 1))
                if u == 0 and later(k):
                    pe.wait_ge(y_out.sem, y_out.at(k - 1, 3))
                if kt == 0 and hg > 0:
                    pe.wait_ge(yT_out.sem, yT_out.at(k, hg))
                for j in range(HG):
                    at = (hg * HG + j) * VC
                    last = nc.tensor.matmul(pvb[PAD * j:PAD * (j + 1), :], V1[:, kt, at:at + PAD],
                                            probs[:, (2 * u + j // 2) % 4, j % 2, :],
                                            start=kt == 0, stop=kt == TT - 1)
                last.then_inc(pv_done.sem, 1)

            def yT_back(k, hg):
                pe.wait_ge(yT_out.sem, yT_out.at(k, hg + 1))
                if hg == 1:
                    pe.wait_ge(negT_out.sem, negT_out.at(k, 1))
                if hg > 1:
                    pe.wait_ge(Y_out.sem, Y_out.at(k, hg))
                for t in range(TT):
                    last = nc.tensor.transpose(M0[:, t * P:(t + 1) * P], yT_sb[:, hg % 2, t * P:(t + 1) * P], ident[:])
                last.then_inc(yT_ready.sem, 1)

            def logits_T(k, v):
                n, u = divmod(v, SUB)
                if v == 0:
                    pe.wait_ge(phi2_out.sem, phi2_out.at(k, 2))
                    if k is not NS:
                        pe.wait_ge(probs_out.sem, probs_out.at(k, wide_pairs(k)))
                    pe.wait_ge(neg_in.sem, neg_in.at(k - 1, TT))
                    pe.wait_ge(y_out.sem, y_out.at(k - 1, 4))
                else:
                    pe.wait_ge(E2_out.sem, E2_out.at(k, v))
                s, m = slice(u * P, (u + 1) * P), slice(n * NT, (n + 1) * NT)
                halves(Fb, ((phi2_h[:, s], xnT_h[:, m]), (phi2_h[:, s], xnT_l[:, m]),
                               (phi2_l[:, s], xnT_h[:, m]), (pick[:, n, :], neg_rows[:]))).then_inc(lgT_ready.sem, 1)

            def combine(k, n, half):
                if half == 0:
                    pe.wait_ge(E2_out.sem, E2_out.at(k, SUB * (n + 1)))
                j = 2 * n + half
                if j == 1 and k is not NS:
                    for e in range(2):
                        pe.wait_ge(D_out[e].sem, D_out[e].at(k, copies(e, NU - 1)))
                if j >= 3:
                    pe.wait_ge(accB_out.sem, accB_out.at(k, j - 2))
                for m in range(2):
                    t = 2 * half + m
                    for u in range(SUB):
                        last = nc.tensor.matmul(o_bank[j % 3][:, m * CZ:(m + 1) * CZ],
                                                E2[:, (SUB * n + u) % 4, t * P:(t + 1) * P], y[:, n, u, :],
                                                start=u == 0, stop=u == SUB - 1)
                last.then_inc(o_done.sem, 1)

            def neg_transpose(k):
                pe.wait_ge(parts_out.sem, parts_out.at(k, 5))
                pe.wait_ge(Y_out.sem, Y_out.at(k, 1))
                nc.tensor.transpose(M0[:].bitcast(BF16)[0:TT * 3 * NB, 0:P],
                                    neg_parts[:].rearrange("p t a b -> p (t a b)"), identb[:]).then_inc(negT_ready.sem, 1)

            def slots(k, pr, ffn2):
                if pr == 0:
                    pe.wait_ge(disp_out.sem, disp_out.at(k, TT))
                if pr < 2 and ffn2:
                    pe.wait_ge(accB_out.sem, accB_out.at(k, 2 * NB - 2 + pr))
                if pr < 2:
                    for e in range(2):
                        pe.wait_ge(D_out[e].sem, D_out[e].at(k, copies(e, NU - 1)))
                else:
                    pe.wait_ge(slots_out.sem, slots_out.at(k, pr - 1))
                for n in range(2):
                    for t in range(TT):
                        last = nc.tensor.matmul(L[pr % 2][:, n * SW:(n + 1) * SW], xn[:, (2 * pr + n) * TT + t, :],
                                                D[:, t, 2 * pr + n, :], start=t == 0, stop=t == TT - 1)
                last.then_inc(slots_ready.sem, 1)

            def experts(k, pr, ffn2):
                pe.wait_ge(slots_out.sem, slots_out.at(k, pr + 1))
                if pr == 0:
                    pe.wait_ge(W_in.sem, W_in.at(k, 1))
                    pe.wait_ge(yT_out.sem, yT_out.at(k, NHG))
                if pr == 1 and ffn2:
                    pe.wait_ge(accB_out.sem, accB_out.at(k, 2 * NB))
                if pr == 1 and not ffn2:
                    pe.wait_ge(probs_out.sem, probs_out.at(k, 2 * NU))
                if pr >= 2:
                    pe.wait_ge(y_out.sem, y_out.at(k, pr - 1))
                for n in range(2):
                    for u in range(SUB):
                        for j in range(P // NP):
                            at = u * P + j * NP
                            last = nc.tensor.matmul(
                                y_bank[pr % 2][j * NP:(j + 1) * NP, (n * SUB + u) * C:(n * SUB + u + 1) * C],
                                slots_sb[:, pr % 2, n, at:at + NP], W_sb[:, u * (P // NP) + j, :], start=True, stop=True)
                last.then_inc(y_ready.sem, 1)

            def attention_transposes(k):
                pe.wait_ge(AO_out.sem, AO_out.at(k, 1))
                for t in range(TT):
                    last = nc.tensor.transpose(M0[:, t * P:(t + 1) * P], AO[:, t, :], ident[:])
                last.then_inc(aoT_ready.sem, 1)

            def project(k):
                pe.wait_ge(AOT_out.sem, AOT_out.at(k, 1))
                for t in range(TT):
                    last = nc.tensor.matmul(M0[:, t * C:(t + 1) * C], AOT[:, t * P:(t + 1) * P], wp[:], start=True, stop=True)
                last.then_inc(proj_ready.sem, 1)

            def ffn2_part(k, n, half):
                if n < NB:
                    logits_T(k, SUB * n + half)
                if n > 0:
                    combine(k, n - 1, half)

            def stage(k, ffn2, ahead):
                pe.wait_ge(stackT_out.sem, stackT_out.at(k, 4))
                for u in range(NU):
                    n = u - FFN2_FROM
                    for half in range(2):
                        scores(k, 2 * u + half)
                        for i in half_of(LOGITS, u, half):
                            logits(k, i)
                        if ffn2 and 0 <= n <= NB:
                            ffn2_part(k, n, half)
                        if u == NU - 1 and half == 0:
                            slots(k, 0, ffn2)
                    if u > 0:
                        pv(k, u - 1)
                    if ahead and 1 <= u <= TT:
                        if u == 1 and later(k):
                            pe.wait_ge(xa_sum.sem, xa_sum.at(k - 1, 1))
                        if u == 1 and not later(k):
                            pe.wait_ge(qkv_out.sem, qkv_out.at(0, TT))
                        qkv_products(k + 1, u - 1)
                    if u == NEG_STEP:
                        neg_transpose(k)
                    if u % TT == 1 and u > TT:
                        if u == TT + 1 and ahead:
                            pe.wait_ge(qkv_out.sem, qkv_out.at(k + 1, TT))
                        yT_back(k, u // TT - 1)
                slots(k, 1, ffn2)
                pv(k, NU - 1)
                slots(k, 2, ffn2)
                yT_back(k, NHG - 1)
                experts(k, 0, ffn2)
                if ahead:
                    stack_transposes(k + 1, 0)
                slots(k, 3, ffn2)
                experts(k, 1, ffn2)
                if ahead:
                    stack_transposes(k + 1, 1)
                experts(k, 2, ffn2)
                if ahead:
                    stack_transposes(k + 1, 2)
                attention_transposes(k)
                experts(k, 3, ffn2)
                if ahead:
                    stack_transposes(k + 1, 3)
                project(k)

            pe.wait_ge(consts.sem, consts.at(0, 2))
            pe.wait_ge(w_in.sem, w_in.at(0, 2))
            for r in range(3):
                last = nc.tensor.transpose(M0[:, r * P:(r + 1) * P], w_stage[:, r, :], ident[:])
            last.then_inc(p_wT.sem, 1)
            nc.tensor.transpose(M1[:, 0:P], wp_stage, ident[:]).then_inc(p_wT.sem, 1)
            for n in range(NB):
                pe.wait_ge(p_xn.sem, p_xn.at(0, TT * (n + 1)))
                if n >= 2:
                    pe.wait_ge(p_Tl.sem, p_Tl.at(0, n - 1))
                for t in range(TT):
                    last = nc.tensor.transpose(L[n % 2][:, t * P:(t + 1) * P], xn[:, n * TT + t, :], ident[:])
                last.then_inc(p_T.sem, 1)
                if n == 1:
                    pe.wait_ge(p_wh.sem, p_wh.at(0, 2))
                    pe.wait_ge(p_wl.sem, p_wl.at(0, 1))
                    pe.wait_ge(p_Tl.sem, p_Tl.at(0, 1))
                if 1 <= n < 1 + TT:
                    qkv_products(0, n - 1)
            pe.wait_ge(consts.sem, consts.at(0, CONSTS))
            for g in range(4):
                stack_transposes(0, g)
            pe.wait_ge(p_Tl.sem, p_Tl.at(0, NB))
            stage(0, False, True)
            with pe.Fori(1, NS - 1) as k:
                stage(k, True, True)
            stage(NS - 1, True, False)
            for n in range(NB + 1):
                for half in range(2):
                    ffn2_part(NS, n, half)

        @block.scalar
        def _(act):
            def copy(dst, src):
                return nc.scalar.activation(dst, src, ACT.Copy)

            def qkv_copy(k, t):
                act.wait_ge(qkv_ready.sem, qkv_ready.at(k, t + 1))
                copy(qkv[:, t, :], M0[:, 0:3 * C]).then_inc(qkv_out.sem, 1)

            def logits_copy(k, i):
                t, pr = divmod(i, NB // 2)
                act.wait_ge(logits_ready.sem, logits_ready.at(k, i + 1))
                copy(D[:, t, 2 * pr:2 * pr + 2, :].rearrange("p b s -> p (b s)"), L[i % 2][:]).then_inc(D_out[0].sem, 1)

            def dispatch_exp(k, t, half):
                if half == 0:
                    act.wait_ge(sub_out.sem, sub_out.at(k, t + 1))
                part = slice(half * NB // 2, (half + 1) * NB // 2)
                nc.scalar.activation(D[:, t, part], D[:, t, part], ACT.Exp).then_inc(E_out.sem, 1)

            def probabilities(k, pair):
                act.wait_ge(scores_ready.sem, scores_ready.at(k, pair + 1))
                if pair >= 4:
                    act.wait_ge(pv_done.sem, pv_done.at(k, pair // 2 - 1))
                nc.scalar.activation(probs[:, pair % 4], (alt if pair < wide_pairs(k) and pair % 2 else sc)[:], ACT.Exp, scale=SCALE).then_inc(probs_out.sem, 1)

            def combine_exp(k, v):
                act.wait_ge(lgT_ready.sem, lgT_ready.at(k, v + 1))
                if v >= 4:
                    act.wait_ge(o_done.sem, o_done.at(k, 2 * (v // SUB) - 2))
                nc.scalar.activation(E2[:, v % 4, :], Fb, ACT.Exp).then_inc(E2_out.sem, 1)

            def stackT_copy(k, g):
                which, pair = divmod(g, 2)
                act.wait_ge(stackT_ready.sem, stackT_ready.at(k, g + 1))
                copy(stackT[:, which, 2 * pair:2 * pair + 2, :].rearrange("p n m -> p (n m)"),
                     stack_bank(k, g).bitcast(F16)).then_inc(stackT_out.sem, 1)

            def yT_copy(k, hg):
                act.wait_ge(pv_done.sem, pv_done.at(k, TT * (hg + 1)))
                if hg >= 2:
                    act.wait_ge(yT_ready.sem, yT_ready.at(k, hg - 1))
                copy(yT_sb[:, hg % 2, :], pvb[:]).then_inc(yT_out.sem, 1)

            def stage(k, ffn2, ahead):
                act.wait_ge(qkv_out.sem, qkv_out.at(k, TT))
                if later(k):
                    act.wait_ge(AO_out.sem, AO_out.at(k - 1, 1))
                copy(V_v, V_in).then_inc(V_out.sem, 1)
                for u in range(NU):
                    n = u - FFN2_FROM
                    for half in range(2):
                        probabilities(k, 2 * u + half)
                        for i in half_of(LOGITS, u, half):
                            if copier(i) == 0:
                                logits_copy(k, i)
                        if ffn2 and 0 <= n < NB:
                            combine_exp(k, SUB * n + half)
                        if u in DISPATCH_EXP:
                            dispatch_exp(k, DISPATCH_EXP[u], half)
                        if half == 1 and u % TT == 0 and u >= TT:
                            yT_copy(k, u // TT - 1)
                for pr in range(4):
                    if pr == 2:
                        yT_copy(k, NHG - 1)
                    if pr == 3 and ahead:
                        stackT_copy(k + 1, 0)
                    act.wait_ge(slots_ready.sem, slots_ready.at(k, pr + 1))
                    if pr >= 2:
                        act.wait_ge(y_ready.sem, y_ready.at(k, pr - 1))
                    copy(slots_sb[:, pr % 2].rearrange("p n s -> p (n s)"), L[pr % 2][:]).then_inc(slots_out.sem, 1)
                if ahead:
                    stackT_copy(k + 1, 1)
                    stackT_copy(k + 1, 2)
                act.wait_ge(aoT_ready.sem, aoT_ready.at(k, 1))
                copy(AOT, M0[:]).then_inc(AOT_out.sem, 1)
                if ahead:
                    stackT_copy(k + 1, 3)
                act.wait_ge(flash_out.sem, flash_out.at(k, 4))
                if ffn2:
                    act.wait_ge(accB_out.sem, accB_out.at(k, 2 * NB))
                nc.scalar.activation(ab[:], ab_log[:], ACT.Exp).then_inc(ab_out.sem, 1)

            act.wait_ge(p_wT.sem, p_wT.at(0, 1))
            copy(wq_h[:], M0[:, 0:3 * C]).then_inc(p_wh.sem, 1)
            act.wait_ge(p_wT.sem, p_wT.at(0, 2))
            copy(wp[:], M1[:, 0:C]).then_inc(p_wh.sem, 1)
            for n in range(NB + 3):
                if n >= 3:
                    m = n - 3
                    act.wait_ge(p_T.sem, p_T.at(0, m + 1))
                    copy(xnT_h[:, m * NT:(m + 1) * NT], L[m % 2][:]).then_inc(p_Th.sem, 1)
                    if 1 <= m < 1 + TT:
                        qkv_copy(0, m - 1)
                if n < NB:
                    act.wait_ge(p_mean.sem, p_mean.at(0, n + 1))
                    for t in range(TT):
                        at = n * TT + t
                        if at >= 4:
                            act.wait_ge(p_sq.sem, p_sq.at(0, at - 3))
                        nc.scalar.activation(dump[:, at % 4, 0:C], x_stage[:, n, t, :], ACT.Square,
                                             bias=ln_neg_mean[:, n, t:t + 1],
                                             accum_out=ln_var[:, n, t:t + 1]).then_inc(p_sq.sem, 1)
            for g in range(4):
                stackT_copy(0, g)
            act.wait_ge(consts.sem, consts.at(0, CONSTS))
            act.wait_ge(p_xn.sem, p_xn.at(0, NB * TT))
            stage(0, False, True)
            with act.Fori(1, NS - 1) as k:
                stage(k, True, True)
            stage(NS - 1, True, False)
            for n in range(NB):
                combine_exp(NS, SUB * n)
                combine_exp(NS, SUB * n + 1)

        @block.vector
        def _(dve):
            def keep_phi(k):
                if later(k - 1):
                    dve.wait_ge(lgT_ready.sem, lgT_ready.at(k - 1, NU))
                nc.vector.tensor_copy(phi2_h[:], phi1_h[:].bitcast(F32)).then_inc(phi2_out.sem, 1)
                nc.vector.tensor_copy(phi2_l[:], phi1_l[:].bitcast(F32)).then_inc(phi2_out.sem, 1)

            def split_phi(k):
                dve.wait_ge(phi_in.sem, phi_in.at(k, 1))
                nc.vector.tensor_copy(phi1_h[:], phi_raw[:]).then_inc(phi1h_out.sem, 1)
                dve.wait_ge(phi1h_out.sem, phi1h_out.at(k, 1))
                nc.vector.tensor_tensor(phi1_l[:], phi_raw[:], phi1_h[:].bitcast(F32), ALU.subtract).then_inc(phi1_out.sem, 1)

            def mean_squares(k):
                dve.wait_ge(qkv_out.sem, qkv_out.at(k, TT))
                qk = qkv[:, :, 0:2 * C]
                sq = work[:].rearrange("p a t c -> p (a t c)").rearrange("p (t c) -> p t c", t=TT)
                nc.vector.tensor_tensor(sq, qk, qk, ALU.mult).then_inc(sq_out.sem, 1)
                dve.wait_ge(sq_out.sem, sq_out.at(k, 1))
                nc.vector.tensor_reduce(mean_sq[:], work[:].rearrange("p a t c -> p (a t c)").rearrange(
                    "p (g d) -> p g d", d=DH), axis=AX.X, op=ALU.add).then_inc(ms_out.sem, 1)
                dve.wait_ge(ms_out.sem, ms_out.at(k, 1))
                nc.vector.tensor_scalar(mean_sq[:], mean_sq[:], 1.0 / DH, RMS_EPS, ALU.mult, ALU.add).then_inc(ms_out.sem, 1)

            def inverse_rms(k):
                dve.wait_ge(ms_out.sem, ms_out.at(k, 2))
                nc.vector.tensor_scalar(rms[:].bitcast(I32), mean_sq[:].bitcast(I32), -0.5, RSQRT_GUESS,
                                        ALU.mult, ALU.add).then_inc(rms_out.sem, 1)
                dve.wait_ge(rms_out.sem, rms_out.at(k, 1))
                nc.vector.tensor_scalar(mean_sq[:], mean_sq[:], -0.5, None, ALU.mult).then_inc(rms_out.sem, 1)
                for n in range(3):
                    dve.wait_ge(rms_out.sem, rms_out.at(k, 3 * n + 2))
                    nc.vector.tensor_tensor(rms_step[:], rms[:], rms[:], ALU.mult).then_inc(rms_out.sem, 1)
                    dve.wait_ge(rms_out.sem, rms_out.at(k, 3 * n + 3))
                    nc.vector.tensor_tensor(rms_step[:], rms_step[:], mean_sq[:], ALU.mult).then_inc(rms_out.sem, 1)
                    dve.wait_ge(rms_out.sem, rms_out.at(k, 3 * n + 4))
                    nc.vector.scalar_tensor_tensor(out=rms[:], in0=rms_step[:], scalar=1.5, in1=rms[:],
                                                   op0=ALU.add, op1=ALU.mult).then_inc(rms_out.sem, 1)

            def split_stack(k, which):
                dve.wait_ge(normed_out.sem, normed_out.at(k, which + 1))
                src = work[:, which].rearrange("p t (h d) -> p (t h) d", d=DH).unsqueeze(2).to_broadcast([P, TT * H, 2, DH])
                hi = stack[:, which, :, 0:2, :] if which == 0 else stack[:, which, :, 0:4:2, :]
                lo = stack[:, which, :, 2:4, :] if which == 0 else stack[:, which, :, 1:4:2, :]
                nc.vector.tensor_copy(hi, src).then_inc(half_out.sem, 1)
                dve.wait_ge(half_out.sem, half_out.at(k, which + 1))
                nc.vector.tensor_tensor(lo, src, hi, ALU.subtract).then_inc(stack_out.sem, 1)

            def qkv_copy(k, t):
                if t == 0:
                    dve.wait_ge(V_out.sem, V_out.at(k - 1, 1))
                    dve.wait_ge(normed_out.sem, normed_out.at(k - 1, 2))
                dve.wait_ge(qkv_ready.sem, qkv_ready.at(k, t + 1))
                nc.vector.tensor_copy(qkv[:, t, :], M0[:, 0:3 * C]).then_inc(qkv_out.sem, 1)

            def logits_copy(k, i):
                t, pr = divmod(i, NB // 2)
                dve.wait_ge(logits_ready.sem, logits_ready.at(k, i + 1))
                nc.vector.tensor_copy(D[:, t, 2 * pr:2 * pr + 2, :].rearrange("p b s -> p (b s)"),
                                      L[i % 2][:]).then_inc(D_out[1].sem, 1)

            def row_maxima(k, h):
                t, half = divmod(h, 2)
                for e in range(2):
                    if copies(e, 2 * h + 1):
                        dve.wait_ge(D_out[e].sem, D_out[e].at(k, copies(e, 2 * h + 1)))
                part = slice(half * NB // 2, (half + 1) * NB // 2)
                nc.vector.tensor_reduce(row_max[:, t, part], D[:, t, part], axis=AX.X, op=ALU.max).then_inc(rmax_out.sem, 1)

            def batch_maxima(k, t):
                nc.vector.tensor_reduce(over_batches[:, t, :], D[:, t].rearrange("p b s -> p s b"),
                                        axis=AX.X, op=ALU.max).then_inc(bmax_out.sem, 1)

            def neg_in_parts(k):
                dve.wait_ge(rmax_out.sem, rmax_out.at(k, 2 * TT))
                nc.vector.tensor_scalar(neg_max[:], row_max[:], -1.0, None, ALU.mult).then_inc(nmax_out.sem, 1)
                dve.wait_ge(nmax_out.sem, nmax_out.at(k, 1))
                nc.vector.tensor_copy(neg_parts[:, :, 0, :], neg_max[:]).then_inc(parts_out.sem, 1)
                dve.wait_ge(parts_out.sem, parts_out.at(k, 1))
                nc.vector.tensor_tensor(neg_rest[:, 0], neg_max[:], neg_parts[:, :, 0, :], ALU.subtract).then_inc(parts_out.sem, 1)
                dve.wait_ge(parts_out.sem, parts_out.at(k, 2))
                nc.vector.tensor_copy(neg_parts[:, :, 1, :], neg_rest[:, 0]).then_inc(parts_out.sem, 1)
                dve.wait_ge(parts_out.sem, parts_out.at(k, 3))
                nc.vector.tensor_tensor(neg_rest[:, 1], neg_rest[:, 0], neg_parts[:, :, 1, :], ALU.subtract).then_inc(parts_out.sem, 1)
                dve.wait_ge(parts_out.sem, parts_out.at(k, 4))
                nc.vector.tensor_copy(neg_parts[:, :, 2, :], neg_rest[:, 1]).then_inc(parts_out.sem, 1)

            def negT_copy(k):
                dve.wait_ge(negT_ready.sem, negT_ready.at(k, 1))
                if later(k):
                    dve.wait_ge(neg_in.sem, neg_in.at(k - 1, TT))
                nc.vector.tensor_copy(negT[:], M0[:].bitcast(BF16)[0:TT * 3 * NB, 0:P]).then_inc(negT_out.sem, 1)

            def batch_sums(k, t):
                dve.wait_ge(E_out.sem, E_out.at(k, 2 * t + 2))
                nc.vector.tensor_reduce(over_batches[:, t, :], D[:, t].rearrange("p b s -> p s b"),
                                        axis=AX.X, op=ALU.add).then_inc(bsum_out.sem, 1)
                dve.wait_ge(bsum_out.sem, bsum_out.at(k, t + 1))
                nc.vector.reciprocal(over_batches[:, t, :], over_batches[:, t, :]).then_inc(brec_out.sem, 1)

            def accumulate(k, n):
                dve.wait_ge(accA_out.sem, accA_out.at(k, n + 1))
                for half in range(2):
                    j = 2 * n + half
                    dve.wait_ge(o_done.sem, o_done.at(k, j + 1))
                    for m in range(2):
                        t = 2 * half + m
                        last = nc.vector.scalar_tensor_tensor(out=acc[:, n, t, :], in0=o_bank[j % 3][:, m * CZ:(m + 1) * CZ],
                                                              scalar=ab[:, 1, t, n:n + 1], in1=acc[:, n, t, :],
                                                              op0=ALU.mult, op1=ALU.add)
                    last.then_inc(accB_out.sem, 1)

            def take_Y(k, hg):
                dve.wait_ge(yT_ready.sem, yT_ready.at(k, hg + 1))
                nc.vector.tensor_copy(Y[:, :, hg * HG:(hg + 1) * HG, :],
                                      M0[:].rearrange("p (t j r) -> p t j r", t=TT, j=HG)[:, :, :, 0:VC]).then_inc(Y_out.sem, 1)

            def v_norms(k):
                dve.wait_ge(vsq_out.sem, vsq_out.at(k, 1))
                nc.vector.tensor_reduce(vv[:], work[:, 0].rearrange("p t (h d) -> p (t h) d", d=DH),
                                        axis=AX.X, op=ALU.add).then_inc(vv_out.sem, 1)
                dve.wait_ge(vv_out.sem, vv_out.at(k, 1))
                nc.vector.tensor_scalar(vv[:], vv[:], NORM_EPS2, None, ALU.max).then_inc(vv_out.sem, 1)
                dve.wait_ge(vv_out.sem, vv_out.at(k, 2))
                nc.vector.reciprocal(vv[:], vv[:]).then_inc(vv_out.sem, 1)

            def finish_attention(k):
                w0 = work[:, 0].rearrange("p t (h d) -> p t h d", d=DH)
                w1 = work[:, 1].rearrange("p t (h d) -> p t h d", d=DH)
                dve.wait_ge(Y_out.sem, Y_out.at(k, NHG))
                dve.wait_ge(vv_out.sem, vv_out.at(k, 3))
                nc.vector.tensor_tensor(w1, Y[:, :, :, 0:DH], V_v, ALU.mult).then_inc(post_out.sem, 1)
                nc.vector.reciprocal(inv_den[:].rearrange("p (t h) -> p t h", t=TT), Y[:, :, :, DH]).then_inc(post_out.sem, 1)
                dve.wait_ge(post_out.sem, post_out.at(k, 1))
                nc.vector.tensor_reduce(dots[:], work[:, 1].rearrange("p t (h d) -> p (t h) d", d=DH),
                                        axis=AX.X, op=ALU.add).then_inc(post_out.sem, 1)
                dve.wait_ge(post_out.sem, post_out.at(k, 3))
                nc.vector.tensor_tensor(dots[:], dots[:], vv[:], ALU.mult).then_inc(post_out.sem, 1)
                dve.wait_ge(post_out.sem, post_out.at(k, 4))
                nc.vector.tensor_tensor(w0, V_v, per_head(dots[:]), ALU.mult).then_inc(post_out.sem, 1)
                dve.wait_ge(post_out.sem, post_out.at(k, 5))
                nc.vector.tensor_tensor(w1, Y[:, :, :, 0:DH], w0, ALU.subtract).then_inc(post_out.sem, 1)
                dve.wait_ge(post_out.sem, post_out.at(k, 6))
                nc.vector.tensor_tensor(AO.rearrange("p t (h d) -> p t h d", d=DH), w1, per_head(inv_den[:]),
                                        ALU.mult).then_inc(AO_out.sem, 1)

            def add_bias(k, pr):
                dve.wait_ge(y_ready.sem, y_ready.at(k, pr + 1))
                if pr == 0:
                    dve.wait_ge(bias_in.sem, bias_in.at(k, SUB))
                nc.vector.tensor_tensor(
                    y[:, 2 * pr:2 * pr + 2, :, 0:C],
                    y_bank[pr % 2][:].rearrange("p (n u e) -> p n u e", n=2, u=SUB),
                    bias_sb[:].unsqueeze(1).to_broadcast([P, 2, SUB, C]),
                    ALU.add).then_inc(y_out.sem, 1)

            def flash(k):
                nc.vector.tensor_tensor(m_new[:], m_run[:], row_max[:], ALU.max).then_inc(flash_out.sem, 1)
                dve.wait_ge(flash_out.sem, flash_out.at(k, 1))
                nc.vector.tensor_tensor(ab_log[:, 0], m_run[:], m_new[:], ALU.subtract).then_inc(flash_out.sem, 1)
                nc.vector.tensor_tensor(ab_log[:, 1], row_max[:], m_new[:], ALU.subtract).then_inc(flash_out.sem, 1)
                dve.wait_ge(flash_out.sem, flash_out.at(k, 2))
                nc.vector.tensor_copy(m_run[:], m_new[:]).then_inc(flash_out.sem, 1)

            def stage(k, ffn2, ahead):
                for u in range(NU):
                    n = u - FFN2_FROM
                    for h in ROW_MAXIMA.get(u, ()):
                        row_maxima(k, h)
                    if u in BATCH_MAXIMA:
                        batch_maxima(k, BATCH_MAXIMA[u])
                    for i in range(sum(LOGITS[:u]), sum(LOGITS[:u + 1])):
                        if copier(i) == 1:
                            logits_copy(k, i)
                    if ahead and 1 <= u <= TT:
                        qkv_copy(k + 1, u - 1)
                    if u == 6:
                        neg_in_parts(k)
                        take_Y(k, 0)
                    if u == 5 and ahead:
                        mean_squares(k + 1)
                    if u == 7 and ahead:
                        inverse_rms(k + 1)
                    if u == NEG_STEP + 1:
                        negT_copy(k)
                    if ffn2 and n >= 2:
                        accumulate(k, n - 2)
                    if u in BATCH_SUMS:
                        batch_sums(k, BATCH_SUMS[u])
                    if u == STACK_STEP and ahead:
                        split_stack(k + 1, 0)
                        split_stack(k + 1, 1)
                    if u in (9, 13):
                        take_Y(k, u // TT - 1)
                    if u == 14:
                        v_norms(k)
                        flash(k)
                        keep_phi(k + 1)
                        if ahead:
                            dve.wait_ge(phi2_out.sem, phi2_out.at(k + 1, 2))
                            dve.wait_ge(logits_ready.sem, logits_ready.at(k, NU))
                            split_phi(k + 1)
                take_Y(k, NHG - 1)
                finish_attention(k)
                for pr in range(4):
                    add_bias(k, pr)
                dve.wait_ge(proj_ready.sem, proj_ready.at(k, 1))
                dve.wait_ge(xa_in.sem, xa_in.at(k, 1))
                nc.vector.tensor_tensor(x_attn[:].rearrange("p t c -> p (t c)"), M0[:],
                                        x_attn[:].rearrange("p t c -> p (t c)"), ALU.add).then_inc(xa_sum.sem, 1)

            def mean(n):
                dve.wait_ge(x_in[n].sem, x_in[n].at(0, 1))
                nc.vector.tensor_reduce(ln_sum[:, n, :], x_stage[:, n], axis=AX.X, op=ALU.add).then_inc(p_sum.sem, 1)
                dve.wait_ge(p_sum.sem, p_sum.at(0, n + 1))
                nc.vector.tensor_scalar(ln_neg_mean[:, n, :], ln_sum[:, n, :], -1.0 / C, None, ALU.mult).then_inc(p_mean.sem, 1)

            def variance(n):
                dve.wait_ge(p_sq.sem, p_sq.at(0, TT * (n + 1)))
                nc.vector.tensor_scalar(ln_var[:, n, :], ln_var[:, n, :], 1.0 / C, LN_EPS, ALU.mult, ALU.add).then_inc(p_eps.sem, 1)

            def normed_x(n):
                dve.wait_ge(p_rstd.sem, p_rstd.at(0, n + 1))
                for t in range(TT):
                    nc.vector.tensor_scalar(xn[:, n * TT + t, :], x_stage[:, n, t, :], ln_neg_mean[:, n, t:t + 1],
                                            ln_rstd[:, n, t:t + 1], ALU.add, ALU.mult).then_inc(p_xn.sem, 1)

            def lower_half(n):
                dve.wait_ge(p_Th.sem, p_Th.at(0, n + 1))
                nc.vector.tensor_tensor(xnT_l[:, n * NT:(n + 1) * NT], L[n % 2][:],
                                        xnT_h[:, n * NT:(n + 1) * NT].bitcast(F32), ALU.subtract).then_inc(p_Tl.sem, 1)

            for n in range(NB + 3):
                if n < NB:
                    mean(n)
                if 1 <= n < NB:
                    variance(n - 1)
                if 2 <= n <= NB + 1:
                    normed_x(n - 2)
                if n == 1:
                    dve.wait_ge(p_wh.sem, p_wh.at(0, 1))
                    nc.vector.tensor_tensor(wq_l[:], M0[:, 0:3 * C], wq_h[:].bitcast(F32), ALU.subtract).then_inc(p_wl.sem, 1)
                if n > NB:
                    split_stack(0, n - NB - 1)
                if n >= 3:
                    lower_half(n - 3)
                if n == NB - 1:
                    mean_squares(0)
                    variance(n)
                    inverse_rms(0)
            split_phi(0)
            dve.wait_ge(consts.sem, consts.at(0, CONSTS))
            stage(0, False, True)
            with dve.Fori(1, NS - 1) as k:
                stage(k, True, True)
            stage(NS - 1, True, False)
            for n in range(NB):
                accumulate(NS, n)
                dve.wait_ge(accB_out.sem, accB_out.at(NS, 2 * n + 2))
                nc.vector.reciprocal(inv_Z[:, n, :], acc[:, n, :, C]).then_inc(inv_Z_out.sem, 1)
                dve.wait_ge(inv_Z_out.sem, n + 1)
                if n == 0:
                    dve.wait_ge(xa_back.sem, xa_back.at(0, 1))
                for t in range(TT):
                    last = nc.vector.scalar_tensor_tensor(out=acc[:, n, t, 0:C], in0=acc[:, n, t, 0:C],
                                                          scalar=inv_Z[:, n, t:t + 1], in1=x_stage[:, n, t, :],
                                                          op0=ALU.mult, op1=ALU.add)
                last.then_inc(total_out.sem, 1)

        @block.gpsimd
        def _(gp):
            def identity(t, at):
                nc.gpsimd.memset(t[:], 0.0).then_inc(consts.sem, 1)
                gp.wait_ge(consts.sem, at)
                nc.gpsimd.affine_select(out=t[:], in_=t[:], compare_op=ALU.not_equal, fill=1.0, base=0,
                                        pattern=[[-1, P]], channel_multiplier=1).then_inc(consts.sem, 1)

            def scale_acc(k, n):
                nc.gpsimd.tensor_tensor(acc[:, n], acc[:, n], ab[:, 0, :, n:n + 1].to_broadcast([P, TT, CZ]),
                                        ALU.mult).then_inc(accA_out.sem, 1)

            def subtract_max(k, t):
                gp.wait_ge(rmax_out.sem, rmax_out.at(k, 2 * t + 2))
                gp.wait_ge(bmax_out.sem, bmax_out.at(k, t + 1))
                nc.gpsimd.tensor_tensor(D[:, t], D[:, t], over_batches[:, t, :].unsqueeze(1).to_broadcast([P, NB, SW]),
                                        ALU.subtract).then_inc(sub_out.sem, 1)

            def dispatch(k, t):
                gp.wait_ge(brec_out.sem, brec_out.at(k, t + 1))
                nc.gpsimd.tensor_tensor(D[:, t], D[:, t], over_batches[:, t, :].unsqueeze(1).to_broadcast([P, NB, SW]),
                                        ALU.mult).then_inc(disp_out.sem, 1)

            def normalise(k):
                gp.wait_ge(rms_out.sem, rms_out.at(k, 11))
                r = rms[:].rearrange("p (t a h) -> p t a h", t=TT, a=2)
                for which in range(2):
                    nc.gpsimd.tensor_tensor(
                        work[:, which].rearrange("p t (h d) -> p t h d", d=DH),
                        qkv[:, :, which * C:(which + 1) * C].rearrange("p t (h d) -> p t h d", d=DH),
                        r[:, :, which, :].unsqueeze(3).to_broadcast([P, TT, H, DH]), ALU.mult).then_inc(normed_out.sem, 1)

            def v_squares(k, ahead):
                if ahead:
                    gp.wait_ge(stack_out.sem, stack_out.at(k + 1, 2))
                gp.wait_ge(V_out.sem, V_out.at(k, 1))
                nc.gpsimd.tensor_tensor(work[:, 0].rearrange("p t (h d) -> p t h d", d=DH), V_v, V_v, ALU.mult).then_inc(vsq_out.sem, 1)

            def stage(k, ffn2, ahead):
                subtract_max(k, 0)
                subtract_max(k, 1)
                subtract_max(k, 2)
                if ffn2:
                    gp.wait_ge(ab_out.sem, ab_out.at(k - 1, 1))
                    for n in range(4):
                        scale_acc(k, n)
                subtract_max(k, 3)
                if ahead:
                    normalise(k + 1)
                dispatch(k, 0)
                if ffn2:
                    for n in range(4, NB):
                        scale_acc(k, n)
                dispatch(k, 1)
                dispatch(k, 2)
                v_squares(k, ahead)
                dispatch(k, 3)

            identity(ident, 1)
            nc.gpsimd.memset(minus_half[:], -0.5).then_inc(consts.sem, 1)
            gp.wait_ge(consts.sem, 3)
            for n in range(NB):
                gp.wait_ge(p_eps.sem, p_eps.at(0, n + 1))
                nc.gpsimd.tensor_tensor(ln_rstd[:, n, :], ln_var[:, n, :], minus_half[:], ALU.pow).then_inc(p_rstd.sem, 1)
                if n == NB - 1:
                    normalise(0)
                if n == 0:
                    identity(ident16, 4)
                if n == 1:
                    identity(identb, 6)
                if n == 2:
                    nc.gpsimd.memset(y[:], 1.0).then_inc(consts.sem, 1)
                    nc.gpsimd.memset(m_run[:], -1e30).then_inc(consts.sem, 1)
                    nc.gpsimd.memset(V1[:], 1.0).then_inc(consts.sem, 1)
                if n in (3, 4):
                    half = slice((n - 3) * NB // 2, (n - 2) * NB // 2)
                    nc.gpsimd.memset(acc[:, half], 0.0).then_inc(consts.sem, 1)
                if n == 5:
                    nc.gpsimd.memset(pick[:], 0.0).then_inc(picks.sem, 1)
                if 5 <= n:
                    q = n - 5
                    gp.wait_ge(picks.sem, picks.at(0, q + 1))
                    last = nc.gpsimd.affine_select(out=pick[:], in_=pick[:], compare_op=ALU.not_equal, fill=1.0, base=-NB * q,
                                                   pattern=[[-1, NB], [0, P]], channel_multiplier=1)
                    last.then_inc(picks.sem if q < 2 else consts.sem, 1)
            stage(0, False, True)
            with gp.Fori(1, NS - 1) as k:
                stage(k, True, True)
            stage(NS - 1, True, False)
            gp.wait_ge(ab_out.sem, ab_out.at(NS - 1, 1))
            for n in range(NB):
                scale_acc(NS, n)


_INS = ["L0_attn_x", "L0_attn_w_qkv", "L0_attn_w_proj", "L0_ffn_phi", "L0_ffn_W", "L0_ffn_b"]


def kernel(**inputs):
    import numpy as _np
    import concourse.bacc as _bacc
    from concourse import mybir as _mybir
    from concourse.bass_utils import run_bass_kernel_spmd as _run

    nc = _bacc.Bacc("TRN2", target_bir_lowering=False, num_devices=1)
    arrays, args = {}, []
    for name in _INS:
        a = _np.ascontiguousarray(inputs[name])
        arrays[f"in_{name}"] = a
        args.append(nc.dram_tensor(f"in_{name}", a.shape, _mybir.dt.from_np(a.dtype), kind="ExternalInput").ap())
    result = nc.dram_tensor("result", (NB, NT, C), F32, kind="ExternalOutput").ap()
    program(nc, *args, result)
    r = _run(nc, [arrays], core_ids=[0])
    return r.results[0]["result"]
```
